# Optimizing a Trainium2 kernel written in Bass

```python
import numpy as np
import jax
import jax.numpy as jnp

def _softmax(x, axis=-1):
    return jax.nn.softmax(x, axis=axis)

def _gelu(x):
    return jax.nn.gelu(x, approximate=True)

def _silu(x):
    return jax.nn.silu(x)

def _sigmoid(x):
    return jax.nn.sigmoid(x)

def _layernorm(x, axis=-1, eps=1e-05):
    m = jnp.mean(x, axis=axis, keepdims=True)
    v = jnp.var(x, axis=axis, keepdims=True)
    return (x - m) / jnp.sqrt(v + eps)

def _scatter_add(tgt, idx, src, axis=0):
    return tgt.at[idx].add(src)

def _segment_sum(src, seg, n):
    return jax.ops.segment_sum(src, seg, n)
kernel_name = 'mk_prb_d1_jaxref_r8_cf0fcd'

def setup_inputs(seed: int=0):
    np.random.seed(seed)
    _w = jnp.asarray

    def _L0_attn_setup():
        import jax, jax.numpy as jnp
        import numpy as np
        N_HEAD = 16
        NEG_INF = jnp.finfo(jnp.float32).min
        key = jax.random.key(seed)
        k1, k2, k3, k4 = jax.random.split(key, 4)
        B, T, C = (4, 256, 128)
        x = jax.random.normal(k1, (B, T, C), dtype=jnp.float32)
        w_attn = jax.random.normal(k2, (C, 3 * C), dtype=jnp.float32) * C ** (-0.5)
        w_proj = jax.random.normal(k3, (C, C), dtype=jnp.float32) * C ** (-0.5)
        decay_raw = jax.random.normal(k4, (N_HEAD,), dtype=jnp.float32)
        return {'x': x, 'w_attn': w_attn, 'w_proj': w_proj, 'decay_raw': decay_raw}
    _L0_attn_in = _L0_attn_setup()

    def _L0_ffn_setup():
        import jax, jax.numpy as jnp
        import numpy as np
        B, T, D = (2, 256, 128)
        E, DFF, TOPK = (8, 512, 2)
        TEMPERATURE = 1.0
        key = jax.random.key(seed)
        k_x, k_w1, k_w2, k_r = jax.random.split(key, 4)
        x = jax.random.normal(k_x, (B, T, D), dtype=jnp.float32)
        W1 = jax.random.normal(k_w1, (E, DFF, D), dtype=jnp.float32) * 0.02
        W2 = jax.random.normal(k_w2, (E, D, DFF), dtype=jnp.float32) * 0.02
        Wr = jax.random.normal(k_r, (E, D), dtype=jnp.float32) * 0.02
        return {'x': x, 'W1': W1, 'W2': W2, 'Wr': Wr}
    _L0_ffn_in = _L0_ffn_setup()
    _d = {'L0_attn_x': _L0_attn_in['x'], 'L0_attn_w_attn': _L0_attn_in['w_attn'], 'L0_attn_w_proj': _L0_attn_in['w_proj'], 'L0_attn_decay_raw': _L0_attn_in['decay_raw'], 'L0_ffn_W1': _L0_ffn_in['W1'], 'L0_ffn_W2': _L0_ffn_in['W2'], 'L0_ffn_Wr': _L0_ffn_in['Wr']}
    _x0 = _d['L0_attn_x']
    _d['L0_attn_x'] = jax.random.normal(jax.random.fold_in(jax.random.key(seed), 1), (8, 512, 128), dtype=_x0.dtype)
    del _x0
    return _d

def reference(L0_attn_x, L0_attn_w_attn, L0_attn_w_proj, L0_attn_decay_raw, L0_ffn_W1, L0_ffn_W2, L0_ffn_Wr):

    def _L0_attn_ref(x, w_attn, w_proj, decay_raw):
        import jax, jax.numpy as jnp
        import numpy as np
        N_HEAD = 16
        NEG_INF = jnp.finfo(jnp.float32).min
        B, T, C = x.shape
        H = N_HEAD
        D = C // H
        qkv = x @ w_attn
        q, k, v = jnp.split(qkv, 3, axis=-1)
        q = q.reshape(B, T, H, D).transpose(0, 2, 1, 3)
        k = k.reshape(B, T, H, D).transpose(0, 2, 1, 3)
        v = v.reshape(B, T, H, D).transpose(0, 2, 1, 3)
        idx = jnp.arange(T)
        causal = jnp.where(idx[None, :] > idx[:, None], NEG_INF, 0.0).astype(jnp.float32)
        decay = jax.nn.softplus(decay_raw)
        dist = jnp.maximum(idx[:, None] - idx[None, :], 0).astype(jnp.float32)
        log1p_dist = jnp.log1p(dist)
        logw = -jnp.log1p(decay[:, None, None] * log1p_dist)
        attn_mask = causal[None, :, :] + logw
        scores = jnp.einsum('bhqd,bhkd->bhqk', q, k) * (1.0 / jnp.sqrt(jnp.float32(D)))
        scores = scores + attn_mask[None]
        att = jax.nn.softmax(scores, axis=-1)
        y = jnp.einsum('bhqk,bhkd->bhqd', att, v)
        y = y.transpose(0, 2, 1, 3).reshape(B, T, C)
        return y @ w_proj

    def _L0_ffn_ref(x, W1, W2, Wr):
        import jax, jax.numpy as jnp
        import numpy as np
        B, T, D = (2, 256, 128)
        E, DFF, TOPK = (8, 512, 2)
        TEMPERATURE = 1.0
        logits = jnp.einsum('btd,ed->bte', x, Wr)
        probs = jax.nn.softmax(logits / TEMPERATURE, axis=-1)
        topk_vals, topk_idx = jax.lax.top_k(probs, TOPK)
        router_weights = topk_vals / topk_vals.sum(-1, keepdims=True)
        one_hot = jax.nn.one_hot(topk_idx, E, dtype=x.dtype)
        gate = jnp.einsum('btk,btke->bte', router_weights, one_hot)
        h = jax.nn.silu(jnp.einsum('btd,efd->btef', x, W1))
        y = jnp.einsum('btef,edf->bted', h, W2)
        out = jnp.einsum('bte,bted->btd', gate, y)
        return out
    x = L0_attn_x
    xn = _layernorm(x, axis=-1)
    x = x + _L0_attn_ref(xn, L0_attn_w_attn, L0_attn_w_proj, L0_attn_decay_raw) + _L0_ffn_ref(xn, L0_ffn_W1, L0_ffn_W2, L0_ffn_Wr)
    return x

_drawn_inputs = setup_inputs


def setup_inputs(seed=0):
    import zlib

    import numpy as np

    out = dict(_drawn_inputs(seed))
    spreads = {}
    factors = {}
    for name, (base, spread) in spreads.items():
        noise = np.random.default_rng([zlib.crc32(name.encode()), seed]).standard_normal(out[name].shape)
        drawn = base * np.exp(spread * noise) if base else spread * noise
        out[name] = jnp.asarray(drawn.astype(out[name].dtype))
    for name, factor in factors.items():
        out[name] = (out[name] * factor).astype(out[name].dtype)
    return out
```

```python
from contextlib import ExitStack

import concourse.bass as bass
from concourse import mybir

F32 = mybir.dt.float32
F32R = mybir.dt.float32r
BF16 = mybir.dt.bfloat16
ALU = mybir.AluOpType
ACT = mybir.ActivationFunctionType
AX = mybir.AxisListType

P = 128
BATCH, SEQ, C = 8, 512, 128
HEADS = 16
HD = C // HEADS
QUADS = 4
QROWS = P // QUADS
GROUPS = HEADS // QUADS
NGROUP = BATCH * GROUPS
TILES = SEQ // P
NTILE = BATCH * TILES
EXPERTS, DFF = 8, 512
FT = DFF // P
EPS = 1e-5
SCALE = float(HD) ** -0.5
NEG = -3.0e38
ROW_HI, ROW_LO, ROW_HI2 = 8, 16, 24

P1_UNITS = 10
P2_UNITS = 5
DVE_UNITS = (4,)
POOL_UNITS = (0, 1, 2, 3)
P1_ALL, P2_ALL = P1_UNITS * NGROUP, P2_UNITS * NGROUP
H_UNITS = 2 * EXPERTS
GAP_STEP = 12

LOOP_FIRST, LOOP_SLOTS, LOOP_TIMES = 5, 8, 3
LAST_SLOT = NGROUP + 5


def slot_steps(n):
    steps = []

    def step(kind, index, limit, *more):
        if 0 <= index < limit:
            steps.append((kind, index - n, *more))

    def per_batch(kind, phase):
        if (n - phase) % GROUPS == 0:
            b = (n - phase) // GROUPS
            if 0 <= b < BATCH and not (kind in ("LN1", "LN2", "XT", "V", "LG") and b == 0):
                steps.append((kind, b * GROUPS - n))

    step("HL", n - 1, NGROUP)
    step("P1", n, NGROUP, 0, 2)
    step("P2", n - 2, NGROUP, 0)
    step("Q", n + 1, NGROUP)
    step("PV", n - 3, NGROUP, 0)
    step("P1", n, NGROUP, 2, 4)
    per_batch("LN1", -3)
    per_batch("LN2", -2)
    step("P2", n - 2, NGROUP, 1)
    step("K", n + 1, NGROUP)
    step("PV", n - 3, NGROUP, 1)
    step("P1", n, NGROUP, 4, 6)
    step("P2", n - 2, NGROUP, 2)
    step("MT", n - 1, NGROUP)
    step("PV", n - 3, NGROUP, 2)
    per_batch("XT", -2)
    per_batch("V", -1)
    step("P1", n, NGROUP, 6, 8)
    step("P2", n - 2, NGROUP, 3)
    step("NT", n - 4, NGROUP)
    step("PV", n - 3, NGROUP, 3)
    step("P1", n, NGROUP, 8, 10)
    per_batch("LG", -1)
    step("P2", n - 2, NGROUP, 4)
    per_batch("YT", 7)
    per_batch("PJ", 8)
    return steps


PROLOGUE = [("LN1", 0), ("LN2", 0), ("XT", 0), ("V", 0), ("LG", 0), ("Q", 0), ("K", 0)]
MISC_KINDS = ("XT", "V", "LG", "Q", "K", "MT", "NT", "YT", "PJ")


def misc_uses():
    uses = {}
    for kind, d in PROLOGUE:
        if kind in MISC_KINDS:
            uses[kind, d] = len(uses)
    for n in range(LAST_SLOT):
        for kind, d, *_ in slot_steps(n):
            if kind in MISC_KINDS:
                uses[kind, n + d] = len(uses)
    return uses


MISC = misc_uses()
MISC_PERIOD = MISC["MT", 8 + 8] - MISC["MT", 8]


class At:

    def __init__(self, i, c):
        if isinstance(i, int):
            self.i, self.c, self.looped = 0, LOOP_SLOTS * i + c, False
        else:
            self.i, self.c, self.looped = i, c, True

    def groups(self, per, more=0):
        k = per * self.c + more
        return self.i * (per * LOOP_SLOTS) + k if self.looped else k

    def batches(self, per, more=0):
        k = per * (self.c // GROUPS) + more
        return self.i * (per * LOOP_SLOTS // GROUPS) + k if self.looped else k

    def misc(self, kind, more=0):
        k = MISC[kind, self.c] + more
        return self.i * MISC_PERIOD + k if self.looped else k

    def first(self):
        return not self.looped and self.c == 0

    @property
    def g(self):
        return self.c % GROUPS

    def ring(self, size):
        return self.c % size

    @property
    def parity(self):
        return self.c // GROUPS % 2


def run_slots(eng, steps):
    def slot(i, c, n):
        for kind, d, *more in slot_steps(n):
            if kind in steps:
                steps[kind](At(i, c + d), *more)

    for kind, d in PROLOGUE:
        if kind in steps:
            steps[kind](At(0, d))
    for n in range(LOOP_FIRST):
        slot(0, n, n)
    with eng.Fori(0, LOOP_TIMES) as i:
        for c in range(LOOP_FIRST, LOOP_FIRST + LOOP_SLOTS):
            slot(i, c, c)
    done = LOOP_FIRST + LOOP_SLOTS * LOOP_TIMES
    for n in range(done, LAST_SLOT):
        slot(0, n, n)


def build(nc, x_in, w_attn, w_proj, decay_raw, w1t, w2t, wrt, out):
    with ExitStack() as ctx:
        def sb(name, shape, dt=F32):
            return ctx.enter_context(nc.sbuf_tensor(name, shape, dt))

        def sem(name):
            return ctx.enter_context(nc.semaphore(name))

        ps1 = ctx.enter_context(nc.psum_tensor("ps1", [P, 2, 512], F32))
        ps2 = ctx.enter_context(nc.psum_tensor("ps2", [P, 2, 2, 512], F32))
        psO = ctx.enter_context(nc.psum_tensor("psO", [P, 512], F32))
        psM = ctx.enter_context(nc.psum_tensor("psM", [P, 512], F32))

        ident = sb("ident", [P, P])
        ident_bf = sb("ident_bf", [P, P], BF16)
        mask_q = sb("mask_q", [P, P], BF16)
        mask_k = sb("mask_k", [P, P], BF16)
        lo_row_q = sb("lo_row_q", [P, 1])
        lo_row_k = sb("lo_row_k", [P, 1])
        one_row_k = sb("one_row_k", [P, 1])
        minus_half = sb("minus_half", [P, TILES])
        w_qkv = sb("w_qkv", [P, 3 * C])
        wq_rows = sb("wq_rows", [P, GROUPS, P])
        wk_rows = sb("wk_rows", [P, GROUPS, P])
        wo = sb("wo", [P, C])
        wr = sb("wr", [P, EXPERTS])
        decay = sb("decay", [P, HEADS])
        decay_in = sb("decay_in", [P, HEADS])
        dec_neg = sb("dec_neg", [P, HEADS])
        dec_abs = sb("dec_abs", [P, HEADS])
        dec_exp = sb("dec_exp", [P, HEADS])
        dec_log = sb("dec_log", [P, HEADS])
        wdist = sb("wdist", [P, HEADS, SEQ])
        w1 = wdist[:, HEADS // 2:, :].rearrange("p h s -> p (h s)")
        w2 = wdist[:, 0:HEADS // 2, :].rearrange("p h s -> p (h s)").rearrange("p (f c) -> p f c", c=C)
        x_all = sb("x_all", [P, NTILE, C])
        xt_all = sb("xt_all", [P, BATCH * SEQ])
        logits = sb("logits", [P, NTILE * EXPERTS])
        stats = sb("stats", [P, TILES, 6])
        mean = sb("mean", [P, 2, TILES])
        between = sb("between", [P, 2, TILES])
        var_eps = sb("var_eps", [P, 2, TILES])
        rstd = sb("rstd", [P, 2, TILES])
        xn = sb("xn", [P, 2, TILES, C])
        xt = sb("xt", [P, 2, SEQ])
        values = sb("values", [P, 2, TILES, HEADS, QROWS])
        y = sb("y", [P, 2, TILES, C])
        yt = sb("yt", [P, SEQ])
        q_rows = sb("q_rows", [P, 4, SEQ], F32R)
        k_rows = sb("k_rows", [P, 2, SEQ], F32R)
        k_heads = [sb(f"k_heads{r}", [P, QUADS, SEQ], F32R) for r in range(4)]
        hi_part = sb("hi_part", [P, SEQ])
        neg_max = sb("neg_max", [P, 2, TILES, QUADS])
        max_cols = sb("max_cols", [P, 2, TILES, QUADS, QROWS])
        probs = sb("probs", [P, 2, P2_UNITS, 1024])
        hidden = probs[:, :, 0:2, :]
        o_rows = sb("o_rows", [P, 2, SEQ])
        rden = sb("rden", [P, TILES, QUADS])

        dist = sb("dist", [P, SEQ])
        log_dist = sb("log_dist", [P, SEQ])
        masked = sb("masked", [P, NTILE, EXPERTS])
        pick1 = sb("pick1", [P, NTILE, EXPERTS])
        pick2 = sb("pick2", [P, NTILE, EXPERTS])
        gates = sb("gates", [P, NTILE, EXPERTS])
        rank = sb("rank", [P, EXPERTS])
        top1 = sb("top1", [P, NTILE])
        top2 = sb("top2", [P, NTILE])
        best = sb("best", [P, NTILE])
        gap_exp = sb("gap_exp", [P, NTILE])
        gate1 = sb("gate1", [P, NTILE])
        gate2 = sb("gate2", [P, NTILE])

        consts_dma = sem("consts_dma")
        x_loaded = sem("x_loaded")
        x_rest_loaded = sem("x_rest_loaded")
        zeroed = sem("zeroed")
        pool_consts = sem("pool_consts")
        w_rows_ready = sem("w_rows_ready")
        decay_ready = sem("decay_ready")
        wdist_log = sem("wdist_log")
        wdist_ready = sem("wdist_ready")
        stats_ready = sem("stats_ready")
        var_ready = sem("var_ready")
        rstd_ready = sem("rstd_ready")
        xn_ready = sem("xn_ready")
        misc_full = sem("misc_full")
        misc_free = sem("misc_free")
        hi_ready = sem("hi_ready")
        k_loaded = sem("k_loaded")
        p1_full = sem("p1_full")
        p1_free = sem("p1_free")
        max_hi = sem("max_hi")
        max_ready = sem("max_ready")
        p2_full = sem("p2_full")
        exp_ready = sem("exp_ready")
        pool_probs = sem("pool_probs")
        dve_probs = sem("dve_probs")
        pv_full = sem("pv_full")
        o_ready = sem("o_ready")
        den_ready = sem("den_ready")
        xt_stored = sem("xt_stored")
        gates_step = sem("gates_step")
        gates_ready = sem("gates_ready")
        out_stored = sem("out_stored")
        experts_dma = sem("experts_dma")
        ident_ready = sem("ident_ready")
        row_masks = sem("row_masks")
        row_masks_step = sem("row_masks_step")
        gap_ready = sem("gap_ready")
        dve_init = sem("dve_init")
        act_init = sem("act_init")


        def unit_heads(w):
            return range(QUADS) if w == 4 else range(2 * (w % 2), 2 * (w % 2) + 2)

        def apply_decay(eng, at, w):
            heads = unit_heads(w)
            unit = probs[:, at.ring(2), w, :].rearrange("p (h k) -> p h k", h=len(heads))
            weights = wdist[:, at.g * QUADS + heads[0]:at.g * QUADS + heads[-1] + 1, :]
            parts = [(0, 384), (384, 512)] if w in (2, 3) else [(0, 1024 // len(heads))]
            for a, b in parts:
                last = eng.tensor_tensor(unit[:, :, a:b], unit[:, :, a:b], weights[:, :, 0:b - a], ALU.mult)
            return last

        N_POOL_CONSTS = 4
        with nc.Block() as block:
            @block.sync
            def _(sp):
                def x_rows(b):
                    return x_in[b].rearrange("(t p) c -> p t c", p=P)

                sp.dma_start(x_all[:, 0:TILES, :], x_rows(0)).then_inc(x_loaded, 16)
                sp.dma_start(w_qkv[:], w_attn).then_inc(consts_dma, 16)
                sp.dma_start(wr[:], wrt).then_inc(consts_dma, 16)
                sp.dma_start(decay_in[:], decay_raw.rearrange("(a h) -> a h", a=1).broadcast_to([P, HEADS])
                             ).then_inc(consts_dma, 16)
                sp.dma_start(wo[:], w_proj).then_inc(consts_dma, 16)
                sp.dma_start(x_all[:, TILES:, :], x_in[1:].rearrange("b (t p) c -> p (b t) c", p=P)
                             ).then_inc(x_rest_loaded, 16)
                sp.wait_ge(zeroed, 4)

                def k_step(at):
                    sp.wait_ge(misc_free, at.misc("K", 1))
                    for quad in range(QUADS):
                        rows = slice(quad * QROWS, (quad + 1) * QROWS)
                        sp.dma_start(k_heads[at.ring(4)][rows, quad, :].bitcast(F32),
                                     k_rows[rows, at.ring(2), :].bitcast(F32)).then_inc(k_loaded, 16)

                def xt_step(at):
                    sp.wait_ge(misc_free, at.misc("XT", 1))
                    sp.dma_start(xt_all[:, bass.ds(at.batches(SEQ), SEQ)],
                                 xt[:, at.parity, :]).then_inc(xt_stored, 16)

                run_slots(sp, {"K": k_step, "XT": xt_step})

                sp.wait_ge(pool_probs, len(POOL_UNITS) * NGROUP)
                sp.wait_ge(dve_probs, NGROUP)
                sp.dma_start(w1, w1t).then_inc(experts_dma, 16)
                sp.dma_start(w2, w2t.rearrange("e (f p) c -> p (e f) c", p=P)).then_inc(experts_dma, 16)

                with sp.Fori(0, BATCH) as b:
                    sp.wait_ge(p1_free, P1_ALL + EXPERTS * b + EXPERTS)
                    sp.dma_start(out[bass.ds(b, 1)].rearrange("b (t p) c -> p (b t) c", p=P),
                                 x_all[:, bass.ds(b * TILES, TILES), :]).then_inc(out_stored, 16)
                sp.wait_ge(out_stored, 16 * BATCH)
                sp.wait_ge(xt_stored, 16 * BATCH)

            @block.gpsimd
            def _(pool):
                nc.gpsimd.memset(ident[:], 1.0).then_inc(pool_consts, 1)
                nc.gpsimd.memset(mask_q[:], 0.0).then_inc(pool_consts, 1)
                nc.gpsimd.memset(mask_k[:], 0.0).then_inc(pool_consts, 1)
                nc.gpsimd.memset(minus_half[:], -0.5).then_inc(pool_consts, 1)
                pool.wait_ge(pool_consts, 4)
                nc.gpsimd.affine_select(out=ident[:], in_=ident[:], compare_op=ALU.is_equal, fill=0.0, base=0,
                                        pattern=[[-1, P]], channel_multiplier=1).then_inc(ident_ready, 1)
                nc.gpsimd.affine_select(out=mask_q[:], in_=mask_q[:], compare_op=ALU.is_ge, fill=NEG, base=0,
                                        pattern=[[-1, P]], channel_multiplier=1).then_inc(ident_ready, 1)
                nc.gpsimd.affine_select(out=mask_k[:], in_=mask_k[:], compare_op=ALU.is_ge, fill=NEG, base=0,
                                        pattern=[[1, P]], channel_multiplier=-1).then_inc(ident_ready, 1)
                nc.gpsimd.iota(dist[:], pattern=[[1, SEQ]], base=0, channel_multiplier=-1,
                               allow_small_or_imprecise_dtypes=True).then_inc(ident_ready, 1)
                nc.gpsimd.iota(rank[:], pattern=[[-1, EXPERTS]], base=EXPERTS, channel_multiplier=0,
                               allow_small_or_imprecise_dtypes=True).then_inc(ident_ready, 1)
                pool.wait_ge(ident_ready, 1)
                nc.gpsimd.tensor_copy(ident_bf[:], ident[:]).then_inc(ident_ready, 1)
                for t in k_heads:
                    nc.gpsimd.memset(t[:].bitcast(F32), 0.0).then_inc(zeroed, 1)

                def ln1_step(at):
                    pool.wait_ge(var_ready, at.batches(3, 3))
                    nc.gpsimd.tensor_tensor(rstd[:, at.parity, :], var_eps[:, at.parity, :], minus_half[:],
                                            ALU.pow).then_inc(rstd_ready, 1)

                def p2_step(at, w):
                    if w not in POOL_UNITS:
                        return
                    if not at.looped and at.c < GROUPS:
                        pool.wait_ge(wdist_ready, at.c + 1)
                    pool.wait_ge(exp_ready, at.groups(P2_UNITS, w + 1))
                    apply_decay(nc.gpsimd, at, w).then_inc(pool_probs, 1)

                run_slots(pool, {"LN1": ln1_step, "P2": p2_step})

            @block.scalar
            def _(act):
                act.wait_ge(dve_init, 2)
                nc.scalar.activation(dec_exp[:], dec_abs[:], ACT.Exp, scale=-1.0).then_inc(act_init, 1)
                act.wait_ge(act_init, 1)
                nc.scalar.activation(dec_log[:], dec_exp[:], ACT.Ln, bias=1.0).then_inc(act_init, 1)
                act.wait_ge(dve_init, 3)
                nc.scalar.activation(log_dist[:], dist[:], ACT.Ln, bias=1.0).then_inc(act_init, 1)
                act.wait_ge(act_init, 3)
                act.wait_ge(row_masks, 2)

                def hi_step(kind, rows, number):
                    def step(at):
                        act.wait_ge(misc_full, at.misc(kind, 1))
                        nc.scalar.activation(hi_part[:].bitcast(F32R), psM[:], ACT.Copy,
                                             scale=rows[:, 0:1]).then_inc(hi_ready, 1)
                    return step

                def decay_weights(g):
                    act.wait_ge(decay_ready, 1)
                    for h in range(g * QUADS, (g + 1) * QUADS):
                        last = nc.scalar.activation(wdist[:, h, :], log_dist[:], ACT.Ln, bias=1.0,
                                                    scale=decay[:, h:h + 1])
                    last.then_inc(wdist_log, 1)
                    act.wait_ge(wdist_log, g + 1)
                    w = wdist[:, g * QUADS:(g + 1) * QUADS, :]
                    nc.scalar.activation(w, w, ACT.Exp, scale=-1.0).then_inc(wdist_ready, 1)

                def k_step(at):
                    hi_step("K", lo_row_k, 2)(at)
                    if not at.looped and at.c in (1, 2):
                        decay_weights(2 * at.c - 2)
                        decay_weights(2 * at.c - 1)

                def xt_step(at):
                    act.wait_ge(misc_full, at.misc("XT", 1))
                    if not at.looped and at.c < 8:
                        pass
                    else:
                        act.wait_ge(xt_stored, at.batches(16, -16))
                    nc.scalar.activation(xt[:, at.parity, :], psM[:], ACT.Copy).then_inc(misc_free, 1)

                def v_step(at):
                    act.wait_ge(misc_full, at.misc("V", 1))
                    nc.scalar.activation(values[:, at.parity, :, :, 0:HD],
                                         psM[:].rearrange("p (t h d) -> p t h d", t=TILES, h=HEADS),
                                         ACT.Copy).then_inc(misc_free, 1)

                def lg_step(at):
                    act.wait_ge(misc_full, at.misc("LG", 1))
                    n = TILES * EXPERTS
                    nc.scalar.activation(logits[:, bass.ds(at.batches(n), n)], psM[:, 0:n],
                                         ACT.Copy).then_inc(misc_free, 1)

                def p2_step(at, w):
                    act.wait_ge(p2_full, at.groups(P2_UNITS, w + 1))
                    nc.scalar.activation(probs[:, at.ring(2), w, :],
                                         ps2[:, (at.c * P2_UNITS + w) % 2].rearrange("p a b -> p (a b)"),
                                         ACT.Exp).then_inc(exp_ready, 1)

                def pv_step(at, chunk):
                    if chunk == 3:
                        act.wait_ge(pv_full, at.groups(1, 1))
                        nc.scalar.activation(o_rows[:, at.ring(2), :], psO[:], ACT.Copy).then_inc(o_ready, 1)

                def yt_step(at):
                    act.wait_ge(misc_full, at.misc("YT", 1))
                    nc.scalar.activation(yt[:], psM[:], ACT.Copy).then_inc(misc_free, 1)

                run_slots(act, {"Q": hi_step("Q", lo_row_q, 1), "K": k_step, "XT": xt_step,
                                "V": v_step, "LG": lg_step, "P2": p2_step, "PV": pv_step, "YT": yt_step})

                act.wait_ge(gates_step, GAP_STEP)
                nc.scalar.activation(gap_exp[:], gap_exp[:], ACT.Exp).then_inc(gap_ready, 1)

                with act.Fori(0, BATCH) as b:
                    for u in range(H_UNITS):
                        act.wait_ge(p2_full, P2_ALL + H_UNITS * b + u + 1)
                        e = u // 2
                        nc.scalar.activation(hidden[:, e % 2, u % 2, :],
                                             ps2[:, u % 2].rearrange("p a b -> p (a b)"),
                                             ACT.Silu).then_inc(exp_ready, 1)

            @block.vector
            def _(dve):
                nc.vector.memset(values[:], 0.0).then_inc(dve_init, 1)
                dve.wait_ge(consts_dma, 16 * 4)
                nc.vector.tensor_scalar(dec_neg[:], decay_in[:], -1.0, None, ALU.mult).then_inc(row_masks_step, 1)
                dve.wait_ge(row_masks_step, 1)
                nc.vector.tensor_tensor(dec_abs[:], decay_in[:], dec_neg[:], ALU.max).then_inc(dve_init, 1)
                dve.wait_ge(ident_ready, 6)
                nc.vector.tensor_scalar(dist[:], dist[:], 0.0, None, ALU.max).then_inc(dve_init, 1)
                cols = ident[:].rearrange("p (q r) -> p q r", q=QUADS)
                for t, a, b in ((lo_row_q, ROW_LO, ROW_HI2), (lo_row_k, ROW_HI2, QROWS), (one_row_k, 0, 2)):
                    nc.vector.tensor_reduce(t[:], cols[:, :, a:b], AX.XY, ALU.add).then_inc(row_masks, 1)
                nc.vector.memset(wq_rows[:], 0.0).then_inc(row_masks_step, 1)
                nc.vector.memset(wk_rows[:], 0.0).then_inc(row_masks_step, 1)
                nc.vector.memset(max_cols[:], 0.0).then_inc(row_masks_step, 1)
                dve.wait_ge(dve_init, 1)
                nc.vector.memset(values[:, :, :, :, HD:HD + 1], 1.0).then_inc(row_masks_step, 1)
                dve.wait_ge(row_masks_step, 5)
                for first in (ROW_HI, ROW_LO, ROW_HI2):
                    for t, w, scale in ((wq_rows, 0, SCALE), (wk_rows, C, 1.0)):
                        nc.vector.tensor_scalar(
                            t[:].rearrange("p g (q r) -> p (g q) r", q=QUADS)[:, :, first:first + HD],
                            w_qkv[:, w:w + C].rearrange("p (h d) -> p h d", h=HEADS),
                            scale, None, ALU.mult).then_inc(w_rows_ready, 1)

                dve.wait_ge(act_init, 2)
                nc.vector.scalar_tensor_tensor(out=decay[:], in0=decay_in[:], scalar=0.0, in1=dec_log[:],
                                               op0=ALU.max, op1=ALU.add).then_inc(decay_ready, 1)

                def ln1_step(at):
                    dve.wait_ge(x_loaded if at.first() else x_rest_loaded, 16)
                    for t in range(TILES):
                        last = nc.vector.bn_stats(stats[:, t, :], x_all[:, bass.ds(at.batches(TILES, t), 1), :]
                                                  .rearrange("p a c -> p (a c)"))
                    last.then_inc(stats_ready, 1)
                    dve.wait_ge(stats_ready, at.batches(1, 1))
                    r = at.parity
                    even, odd = stats[:, :, 0:3], stats[:, :, 3:6]
                    v = nc.vector
                    v.tensor_tensor(mean[:, r, :], even[:, :, 1], odd[:, :, 1], ALU.add)
                    v.tensor_tensor(between[:, r, :], even[:, :, 1], odd[:, :, 1], ALU.subtract)
                    v.tensor_tensor(var_eps[:, r, :], even[:, :, 2], odd[:, :, 2], ALU.add).then_inc(var_ready, 1)
                    dve.wait_ge(var_ready, at.batches(3, 1))
                    v.tensor_scalar(mean[:, r, :], mean[:, r, :], 0.5, None, ALU.mult)
                    v.tensor_tensor(between[:, r, :], between[:, r, :], between[:, r, :], ALU.mult)
                    v.tensor_scalar(var_eps[:, r, :], var_eps[:, r, :], 1.0 / C, EPS, ALU.mult,
                                    ALU.add).then_inc(var_ready, 1)
                    dve.wait_ge(var_ready, at.batches(3, 2))
                    v.scalar_tensor_tensor(out=var_eps[:, r, :], in0=between[:, r, :], scalar=0.25,
                                           in1=var_eps[:, r, :], op0=ALU.mult,
                                           op1=ALU.add).then_inc(var_ready, 1)

                def ln2_step(at):
                    dve.wait_ge(rstd_ready, at.batches(1, 1))
                    for t in range(TILES):
                        last = nc.vector.tensor_scalar(
                            xn[:, at.parity, t, :],
                            x_all[:, bass.ds(at.batches(TILES, t), 1), :].rearrange("p a c -> p (a c)"),
                            mean[:, at.parity, t:t + 1], rstd[:, at.parity, t:t + 1], ALU.subtract, ALU.mult)
                    last.then_inc(xn_ready, 1)

                def q_step(at):
                    dve.wait_ge(hi_ready, at.groups(2, 1))
                    nc.vector.tensor_tensor(q_rows[:, at.ring(4), :], psM[:], hi_part[:],
                                            ALU.subtract).then_inc(misc_free, 1)

                def k_step(at):
                    dve.wait_ge(hi_ready, at.groups(2, 2))
                    nc.vector.scalar_tensor_tensor(out=k_rows[:, at.ring(2), :], in0=psM[:],
                                                   scalar=one_row_k[:, 0:1], in1=hi_part[:], op0=ALU.add,
                                                   op1=ALU.subtract).then_inc(misc_free, 1)

                def p1_step(at, u0, u1):
                    for u in range(u0, u1):
                        bank = ps1[:, u % 2]
                        r = at.ring(2)
                        dve.wait_ge(p1_full, at.groups(P1_UNITS, u + 1))
                        pair, v = u // 5, u % 5
                        if v < 2:
                            todo = [(bank[:, 0:512], neg_max[:, r, 3, 2 * pair + v:2 * pair + v + 1])]
                        elif v < 4:
                            q = 2 * pair + v - 2
                            todo = [(bank[:, 0:384], neg_max[:, r, 2, q:q + 1]),
                                    (bank[:, 384:512], neg_max[:, r, 0, q:q + 1])]
                        else:
                            todo = [(bank.rearrange("p (h k) -> p h k", h=2),
                                     neg_max[:, r, 1, 2 * pair:2 * pair + 2])]
                        for src, dst in todo:
                            last = nc.vector.tensor_reduce(dst, src, AX.X, ALU.max, negate=True)
                        last.then_inc(p1_free, 1)

                def hl_step(at):
                    dve.wait_ge(p1_free, at.groups(P1_UNITS, P1_UNITS))
                    r = at.ring(2)
                    hi = max_cols[:, r, :, :, 0]
                    nc.vector.tensor_copy(hi.bitcast(F32R), neg_max[:, r]).then_inc(max_hi, 1)
                    dve.wait_ge(max_hi, at.groups(1, 1))
                    nc.vector.tensor_tensor(max_cols[:, r, :, :, 1], neg_max[:, r], hi,
                                            ALU.subtract).then_inc(max_ready, 1)

                def mt_step(at):
                    dve.wait_ge(misc_full, at.misc("MT", 1))
                    q = q_rows[:, at.ring(4), :]
                    nc.vector.tensor_tensor(q, psM[:], q.bitcast(F32), ALU.add).then_inc(misc_free, 1)

                def p2_step(at, w):
                    if w in DVE_UNITS:
                        if not at.looped and at.c < GROUPS:
                            dve.wait_ge(wdist_ready, at.c + 1)
                        dve.wait_ge(exp_ready, at.groups(P2_UNITS, 5))
                        apply_decay(nc.vector, at, 4).then_inc(dve_probs, 1)

                def nt_step(at):
                    dve.wait_ge(misc_full, at.misc("NT", 1))
                    o = psM[:].rearrange("p (t q r) -> p t q r", t=TILES, q=QUADS)
                    nc.vector.reciprocal(rden[:], o[:, :, :, HD]).then_inc(den_ready, 1)
                    dve.wait_ge(den_ready, at.groups(1, 1))
                    c0 = at.g * QUADS * HD
                    nc.vector.tensor_tensor(
                        y[:, at.parity, :, c0:c0 + QUADS * HD].rearrange("p t (q d) -> p t q d", q=QUADS),
                        o[:, :, :, 0:HD],
                        rden[:].rearrange("p t (q a) -> p t q a", a=1).broadcast_to([P, TILES, QUADS, HD]),
                        ALU.mult).then_inc(misc_free, 1)

                def pj_step(at):
                    dve.wait_ge(misc_full, at.misc("PJ", 1))
                    x = x_all[:, bass.ds(at.batches(TILES), TILES), :]
                    nc.vector.tensor_tensor(x, psM[:].rearrange("p (t c) -> p t c", t=TILES), x,
                                            ALU.add).then_inc(misc_free, 1)

                run_slots(dve, {"LN1": ln1_step, "LN2": ln2_step, "Q": q_step, "K": k_step,
                                "P1": p1_step, "HL": hl_step, "MT": mt_step, "P2": p2_step, "NT": nt_step,
                                "PJ": pj_step})

                done = [0]

                def step(instruction):
                    done[0] += 1
                    instruction.then_inc(gates_step, 1)
                    dve.wait_ge(gates_step, done[0])

                v = nc.vector
                lg = logits[:].rearrange("p (t e) -> p t e", e=EXPERTS)

                def wide(t):
                    return t[:].rearrange("p (t a) -> p t a", a=1).broadcast_to([P, NTILE, EXPERTS])

                ranks = rank[:].rearrange("p (a e) -> p a e", a=1).broadcast_to([P, NTILE, EXPERTS])
                dve.wait_ge(misc_free, len(MISC))

                def first_of_best(src, top, pick):
                    step(v.tensor_reduce(top[:], src, AX.X, ALU.max))
                    step(v.tensor_tensor(pick[:], src, wide(top), ALU.is_equal))
                    step(v.tensor_tensor(pick[:], pick[:], ranks, ALU.mult))
                    step(v.tensor_reduce(best[:], pick[:], AX.X, ALU.max))
                    step(v.tensor_tensor(pick[:], pick[:], wide(best), ALU.is_equal))

                first_of_best(lg, top1, pick1)
                step(v.scalar_tensor_tensor(out=masked[:], in0=pick1[:], scalar=NEG, in1=lg,
                                            op0=ALU.mult, op1=ALU.add))
                first_of_best(masked[:], top2, pick2)
                step(v.tensor_tensor(gap_exp[:], top2[:], top1[:], ALU.subtract))
                assert done[0] == GAP_STEP
                dve.wait_ge(gap_ready, 1)
                step(v.tensor_scalar(gate1[:], gap_exp[:], 1.0, None, ALU.add))
                step(v.reciprocal(gate1[:], gate1[:]))
                step(v.tensor_tensor(gate2[:], gate1[:], gap_exp[:], ALU.mult))
                step(v.tensor_tensor(pick1[:], pick1[:], wide(gate1), ALU.mult))
                step(v.tensor_tensor(pick2[:], pick2[:], wide(gate2), ALU.mult))
                step(v.tensor_tensor(gates[:], pick1[:], pick2[:], ALU.add))

                with dve.Fori(0, BATCH) as b:
                    for e in range(EXPERTS):
                        dve.wait_ge(p1_full, P1_ALL + EXPERTS * b + e + 1)
                        dve.wait_ge(p1_free, P1_ALL + EXPERTS * b + e)
                        for t in range(TILES):
                            x = x_all[:, bass.ds(b * TILES + t, 1), :].rearrange("p a c -> p (a c)")
                            gate = gates[:, bass.ds(b * TILES + t, 1), e]
                            last = v.scalar_tensor_tensor(out=x, in0=ps1[:, e % 2, t * C:(t + 1) * C],
                                                          scalar=gate, in1=x, op0=ALU.mult, op1=ALU.add)
                        last.then_inc(p1_free, 1)

            @block.tensor
            def _(pe):
                pe.wait_ge(ident_ready, 6)
                pe.wait_ge(w_rows_ready, 6)
                mm = nc.tensor.matmul

                def misc_use(at, kind):
                    if MISC[kind, at.c] or at.looped:
                        pe.wait_ge(misc_free, at.misc(kind))

                def transposes(src):
                    for t in range(TILES):
                        last = nc.tensor.transpose(psM[:, t * P:(t + 1) * P], src(t), ident[:])
                    last.then_inc(misc_full, 1)

                def xt_step(at):
                    misc_use(at, "XT")
                    pe.wait_ge(xn_ready, at.batches(1, 1))
                    transposes(lambda t: xn[:, at.parity, t, :])

                def v_step(at):
                    misc_use(at, "V")
                    for t in range(TILES):
                        last = mm(psM[:, t * C:(t + 1) * C], xt[:, at.parity, t * P:(t + 1) * P],
                                  w_qkv[:, 2 * C:3 * C], start=True, stop=True)
                    last.then_inc(misc_full, 1)

                def lg_step(at):
                    misc_use(at, "LG")
                    for t in range(TILES):
                        last = mm(psM[:, t * EXPERTS:(t + 1) * EXPERTS], xt[:, at.parity, t * P:(t + 1) * P],
                                  wr[:], start=True, stop=True)
                    last.then_inc(misc_full, 1)

                def rows_step(kind, w):
                    def step(at):
                        misc_use(at, kind)
                        mm(psM[:], w[:, at.g, :], xt[:, at.parity, :], start=True, stop=True).then_inc(misc_full, 1)
                    return step

                def p1_step(at, u0, u1):
                    q = q_rows[:, at.ring(4), :]
                    k = k_heads[at.ring(4)]

                    def scores(dst, tile, quad):
                        n = (tile + 1) * P
                        mm(dst[:, 0:n], q[:, tile * P:n], k[:, quad, 0:n], start=True, stop=False)
                        return mm(dst[:, n - P:n], ident_bf[:], mask_q[:], start=False, stop=True)

                    if u0 == 0:
                        pe.wait_ge(misc_free, at.misc("K", 1))
                        pe.wait_ge(k_loaded, at.groups(64, 64))
                    for u in range(u0, u1):
                        if at.looped or at.c * P1_UNITS + u >= 2:
                            pe.wait_ge(p1_free, at.groups(P1_UNITS, u - 1))
                        bank = ps1[:, u % 2]
                        pair, v = u // 5, u % 5
                        if v < 2:
                            last = scores(bank, 3, 2 * pair + v)
                        elif v < 4:
                            scores(bank[:, 0:384], 2, 2 * pair + v - 2)
                            last = scores(bank[:, 384:512], 0, 2 * pair + v - 2)
                        else:
                            scores(bank[:, 0:256], 1, 2 * pair)
                            last = scores(bank[:, 256:512], 1, 2 * pair + 1)
                        last.then_inc(p1_full, 1)

                def mt_step(at):
                    misc_use(at, "MT")
                    pe.wait_ge(max_ready, at.groups(1, 1))
                    transposes(lambda t: max_cols[:, at.ring(2), t].rearrange("p q r -> p (q r)"))

                def p2_step(at, w):
                    q = q_rows[:, at.ring(4), :]
                    k = k_heads[at.ring(4)]
                    if w == 0:
                        pe.wait_ge(misc_free, at.misc("MT", 1))
                    if at.looped or at.c * P2_UNITS + w >= 2:
                        pe.wait_ge(exp_ready, at.groups(P2_UNITS, w - 1))
                    pair = ps2[:, (at.c * P2_UNITS + w) % 2]

                    def scores(dst, tile, quad):
                        a = tile * P
                        mm(dst, k[:, quad, a:a + P], q[:, a:], start=True, stop=False)
                        return mm(dst[:, 0:P], ident_bf[:], mask_k[:], start=False, stop=True)

                    for s, quad in enumerate(unit_heads(w)):
                        if w < 2:
                            last = scores(pair[:, s, :], 0, quad)
                        elif w < 4:
                            scores(pair[:, s, 0:384], 1, quad)
                            last = scores(pair[:, s, 384:512], 3, quad)
                        else:
                            last = scores(pair[:, s // 2, s % 2 * 256:s % 2 * 256 + 256], 2, quad)
                    last.then_inc(p2_full, 1)

                def pv_step(at, chunk):
                    if chunk == 0 and (at.looped or at.c > 0):
                        pe.wait_ge(o_ready, at.groups(1))
                    if chunk == 3:
                        pe.wait_ge(dve_probs, at.groups(1, 1))
                    else:
                        pe.wait_ge(pool_probs, at.groups(4, 2 if chunk == 0 else 4))
                    tile = (0, 1, 3, 2)[chunk]
                    for quad in range(QUADS):
                        unit, a, n = {0: (quad // 2, quad % 2 * 512, 512), 1: (2 + quad // 2, quad % 2 * 512, 384),
                                      3: (2 + quad // 2, quad % 2 * 512 + 384, 128), 2: (4, quad * 256, 256)}[tile]
                        last = mm(psO[quad * QROWS:(quad + 1) * QROWS, tile * P:],
                                  values[:, at.parity, tile, at.g * QUADS + quad, :],
                                  probs[:, at.ring(2), unit, a:a + n], start=(chunk == 0), stop=(chunk == 3))
                    if chunk == 3:
                        last.then_inc(pv_full, 1)

                def nt_step(at):
                    misc_use(at, "NT")
                    pe.wait_ge(o_ready, at.groups(1, 1))
                    transposes(lambda t: o_rows[:, at.ring(2), t * P:(t + 1) * P])

                def yt_step(at):
                    misc_use(at, "YT")
                    transposes(lambda t: y[:, at.parity, t, :])

                def pj_step(at):
                    misc_use(at, "PJ")
                    for t in range(TILES):
                        last = mm(psM[:, t * C:(t + 1) * C], yt[:, t * P:(t + 1) * P], wo[:], start=True, stop=True)
                    last.then_inc(misc_full, 1)

                run_slots(pe, {"XT": xt_step, "V": v_step, "LG": lg_step, "Q": rows_step("Q", wq_rows),
                               "K": rows_step("K", wk_rows), "P1": p1_step, "MT": mt_step, "P2": p2_step,
                               "PV": pv_step, "NT": nt_step, "YT": yt_step, "PJ": pj_step})

                pe.wait_ge(experts_dma, 32)
                pe.wait_ge(xt_stored, 16 * BATCH)

                with pe.Fori(0, BATCH) as b:
                    tokens = xt_all[:, bass.ds(b * SEQ, SEQ)]

                    def up(e):
                        for u in range(2):
                            k = 2 * e + u
                            pe.wait_ge(exp_ready, P2_ALL + H_UNITS * b + k - 1)
                            for s in range(2):
                                f = e * FT + 2 * u + s
                                last = mm(ps2[:, u, s, :], w1[:, f * P:(f + 1) * P], tokens, start=True, stop=True)
                            last.then_inc(p2_full, 1)

                    def down(e):
                        pe.wait_ge(exp_ready, P2_ALL + H_UNITS * b + 2 * e + 2)
                        pe.wait_ge(p1_free, P1_ALL + EXPERTS * b + e - 1)
                        for t in range(TILES):
                            for f in range(FT):
                                h = hidden[:, e % 2, f // 2, f % 2 * 512 + t * P:f % 2 * 512 + (t + 1) * P]
                                last = mm(ps1[:, e % 2, t * C:(t + 1) * C], h, w2[:, e * FT + f, :],
                                          start=(f == 0), stop=(f == FT - 1))
                        last.then_inc(p1_full, 1)

                    up(0)
                    for e in range(EXPERTS):
                        if e + 1 < EXPERTS:
                            up(e + 1)
                        down(e)


def kernel(L0_attn_x, L0_attn_w_attn, L0_attn_w_proj, L0_attn_decay_raw, L0_ffn_W1, L0_ffn_W2, L0_ffn_Wr):
    import numpy as np
    import concourse.bacc as bacc
    from concourse.bass_utils import run_bass_kernel_spmd

    nc = bacc.Bacc("TRN2", target_bir_lowering=False, num_devices=1)
    arrays = {
        "x": np.asarray(L0_attn_x),
        "w_attn": np.asarray(L0_attn_w_attn),
        "w_proj": np.asarray(L0_attn_w_proj),
        "decay_raw": np.asarray(L0_attn_decay_raw),
        "w1t": np.asarray(L0_ffn_W1).transpose(2, 0, 1).reshape(C, EXPERTS * DFF),
        "w2t": np.asarray(L0_ffn_W2).transpose(0, 2, 1),
        "wrt": np.asarray(L0_ffn_Wr).T,
    }
    arrays = {k: np.ascontiguousarray(v) for k, v in arrays.items()}
    args = [nc.dram_tensor(k, v.shape, mybir.dt.from_np(v.dtype), kind="ExternalInput").ap() for k, v in arrays.items()]
    out = nc.dram_tensor("out", (BATCH, SEQ, C), F32, kind="ExternalOutput").ap()
    build(nc, *args, out)
    return run_bass_kernel_spmd(nc, [arrays], core_ids=[0]).results[0]["out"]
```

```python
from contextlib import ExitStack

import concourse.bass as bass
from concourse import mybir

F32 = mybir.dt.float32
F32R = mybir.dt.float32r
I32 = mybir.dt.int32
U32 = mybir.dt.uint32
BF16 = mybir.dt.bfloat16
ALU = mybir.AluOpType
ACT = mybir.ActivationFunctionType
AX = mybir.AxisListType

P = 128
BATCH, SEQ, C = 8, 512, 128
HEADS = 16
HD = C // HEADS
QUADS = 4
QROWS = P // QUADS
GROUPS = HEADS // QUADS
NGROUP = BATCH * GROUPS
TILES = SEQ // P
NTILE = BATCH * TILES
EXPERTS, DFF = 8, 512
FT = DFF // P
EPS = 1e-5
SCALE = float(HD) ** -0.5
NEG = -3.0e38
ROW_HI, ROW_LO, ROW_HI2 = 8, 16, 24

P1_UNITS = 10
P2_UNITS = 5
DVE_UNITS = (4,)
POOL_UNITS = (0, 1, 2, 3)
P1_ALL, P2_ALL = P1_UNITS * NGROUP, P2_UNITS * NGROUP
TOPK = 2
SLOTS_USED = (BATCH * SEQ * TOPK + EXPERTS * (P - 1)) // P
SLOTS = -(-SLOTS_USED // 4) * 4
ROW = C + 2
NOWHERE = 1 << 20
PICKS_STEP, GAP_STEP = 12, 13
TWO23 = 8388608.0

LOOP_FIRST, LOOP_SLOTS, LOOP_TIMES = 5, 8, 3
LAST_SLOT = NGROUP + 5


def slot_steps(n):
    steps = []

    def step(kind, index, limit, *more):
        if 0 <= index < limit:
            steps.append((kind, index - n, *more))

    def per_batch(kind, phase):
        if (n - phase) % GROUPS == 0:
            b = (n - phase) // GROUPS
            if 0 <= b < BATCH and not (kind in ("XT", "V") and b == 0) and not (kind == "XT" and b == 1):
                steps.append((kind, b * GROUPS - n))

    step("HL", n - 1, NGROUP)
    step("P1", n, NGROUP, 0, 2)
    step("P2", n - 2, NGROUP, 0)
    step("Q", n + 1, NGROUP)
    step("PV", n - 3, NGROUP, 0)
    step("P1", n, NGROUP, 2, 4)
    step("P2", n - 2, NGROUP, 1)
    step("K", n + 1, NGROUP)
    step("PV", n - 3, NGROUP, 1)
    step("P1", n, NGROUP, 4, 6)
    step("P2", n - 2, NGROUP, 2)
    step("MT", n - 1, NGROUP)
    step("PV", n - 3, NGROUP, 2)
    per_batch("XT", -2)
    per_batch("V", -1)
    step("P1", n, NGROUP, 6, 8)
    step("P2", n - 2, NGROUP, 3)
    step("NT", n - 4, NGROUP)
    step("PV", n - 3, NGROUP, 3)
    step("P1", n, NGROUP, 8, 10)
    step("P2", n - 2, NGROUP, 4)
    per_batch("YT", 7)
    per_batch("PJ", 8)
    return steps


PROLOGUE = [("V", 0), ("Q", 0), ("K", 0)]
MISC_KINDS = ("V", "Q", "K", "MT", "NT", "YT", "PJ")


SECOND_PICK_SLOT = 3
START_ORDER = [*range(2, BATCH), 0, 1]


def misc_uses():
    uses = {}
    for kind, d in PROLOGUE:
        if kind in MISC_KINDS:
            uses[kind, d] = len(uses)
    for n in range(LAST_SLOT):
        for kind, d, *_ in slot_steps(n):
            if kind in MISC_KINDS:
                uses[kind, n + d] = len(uses)
    return uses


MISC = misc_uses()
MISC_PERIOD = MISC["MT", 8 + 8] - MISC["MT", 8]


class At:

    def __init__(self, i, c):
        if isinstance(i, int):
            self.i, self.c, self.looped = 0, LOOP_SLOTS * i + c, False
        else:
            self.i, self.c, self.looped = i, c, True

    def groups(self, per, more=0):
        k = per * self.c + more
        return self.i * (per * LOOP_SLOTS) + k if self.looped else k

    def batches(self, per, more=0):
        k = per * (self.c // GROUPS) + more
        return self.i * (per * LOOP_SLOTS // GROUPS) + k if self.looped else k

    def misc(self, kind, more=0):
        k = MISC[kind, self.c] + more
        return self.i * MISC_PERIOD + k if self.looped else k

    def misc_before(self, kind, groups, more=0):
        k = MISC[kind, self.c - groups] + more
        return self.i * MISC_PERIOD + k if self.looped else k

    def first(self):
        return not self.looped and self.c == 0

    @property
    def g(self):
        return self.c % GROUPS

    def ring(self, size):
        return self.c % size

    @property
    def parity(self):
        return self.c // GROUPS % 2


def run_slots(eng, steps):
    def slot(i, c, n):
        for kind, d, *more in slot_steps(n):
            if kind in steps:
                steps[kind](At(i, c + d), *more)

    for kind, d in PROLOGUE:
        if kind in steps:
            steps[kind](At(0, d))
    for n in range(LOOP_FIRST):
        slot(0, n, n)
    with eng.Fori(0, LOOP_TIMES) as i:
        for c in range(LOOP_FIRST, LOOP_FIRST + LOOP_SLOTS):
            slot(i, c, c)
    done = LOOP_FIRST + LOOP_SLOTS * LOOP_TIMES
    for n in range(done, LAST_SLOT):
        slot(0, n, n)


def build(nc, x_in, w_attn, w_proj, decay_raw, w1t, w2t, wrt, out):
    with ExitStack() as ctx:
        def sb(name, shape, dt=F32):
            return ctx.enter_context(nc.sbuf_tensor(name, shape, dt))

        def sem(name):
            return ctx.enter_context(nc.semaphore(name))

        xt_dram = nc.dram_tensor("xt_dram", (BATCH - 2, P, SEQ), F32).ap()
        rows_dram = nc.dram_tensor("rows_dram", (SLOTS * P, ROW), F32).ap()
        picked_dram = nc.dram_tensor("picked_dram", (BATCH * SEQ * TOPK, C), F32).ap()

        ps1 = ctx.enter_context(nc.psum_tensor("ps1", [P, 2, 512], F32))
        ps2 = ctx.enter_context(nc.psum_tensor("ps2", [P, 2, 2, 512], F32))
        psO = ctx.enter_context(nc.psum_tensor("psO", [P, 512], F32))
        psM = ctx.enter_context(nc.psum_tensor("psM", [P, 512], F32))

        ident = sb("ident", [P, P])
        ident_bf = sb("ident_bf", [P, P], BF16)
        mask_q = sb("mask_q", [P, P], BF16)
        mask_k = sb("mask_k", [P, P], BF16)
        lo_row_q = sb("lo_row_q", [P, 1])
        lo_row_k = sb("lo_row_k", [P, 1])
        one_row_k = sb("one_row_k", [P, 1])
        minus_half = sb("minus_half", [P, NTILE])
        w_qkv = sb("w_qkv", [P, 3 * C])
        wq_rows = sb("wq_rows", [P, GROUPS, P])
        wk_rows = sb("wk_rows", [P, GROUPS, P])
        wo = sb("wo", [P, C])
        wr = sb("wr", [P, EXPERTS])
        decay = sb("decay", [P, HEADS])
        decay_in = sb("decay_in", [P, HEADS])
        dec_neg = sb("dec_neg", [P, HEADS])
        dec_abs = sb("dec_abs", [P, HEADS])
        dec_exp = sb("dec_exp", [P, HEADS])
        dec_log = sb("dec_log", [P, HEADS])
        wdist = sb("wdist", [P, HEADS, SEQ])
        w1 = wdist[:, HEADS // 2:, :].rearrange("p h s -> p (h s)")
        w2 = wdist[:, 0:HEADS // 2, :].rearrange("p h s -> p (h s)")
        x_all = sb("x_all", [P, NTILE, C])
        xn_all = sb("xn_all", [P, NTILE, ROW])
        logits = sb("logits", [P, NTILE * EXPERTS])
        mean = sb("mean", [P, NTILE])
        between = sb("between", [P, NTILE])
        var_eps = sb("var_eps", [P, NTILE])
        rstd = sb("rstd", [P, NTILE])
        xt = sb("xt", [P, 2, SEQ])
        values = sb("values", [P, 2, TILES, HEADS, QROWS])
        y = sb("y", [P, 2, TILES, C])
        yt = sb("yt", [P, SEQ])
        q_rows = sb("q_rows", [P, 4, SEQ], F32R)
        k_rows = sb("k_rows", [P, 2, SEQ], F32R)
        k_heads = [sb(f"k_heads{r}", [P, QUADS, SEQ], F32R) for r in range(4)]
        hi_part = sb("hi_part", [P, SEQ])
        neg_max = sb("neg_max", [P, 2, TILES, QUADS])
        max_cols = sb("max_cols", [P, 2, TILES, QUADS, QROWS])
        probs = sb("probs", [P, 2, P2_UNITS, 1024])
        start_used = [0]

        def early(*shape):
            n = 1
            for k in shape:
                n *= k
            a = start_used[0]
            start_used[0] += n
            part = probs[:].rearrange("p a u k -> p (a u k)")[:, a:a + n]
            return part.rearrange("p (a b) -> p a b", b=shape[1]) if len(shape) == 2 else part

        ones = early(P)
        before = early(P)
        stats = early(NTILE, 6)
        dist = early(SEQ)
        log_dist = early(SEQ)
        masked, pick1, pick2 = early(NTILE, EXPERTS), early(NTILE, EXPERTS), early(NTILE, EXPERTS)
        sums_a, sums_b = early(NTILE, EXPERTS), early(NTILE, EXPERTS)
        slot_no = early(SLOTS)
        past = early(SLOTS, EXPERTS)
        slot_expert = early(SLOTS)
        picked = probs[:].rearrange("p a u k -> p (a u k)")[:, 0:NTILE * TOPK * C].rearrange(
            "p (t k c) -> p t k c", k=TOPK, c=C)
        hidden, hidden_t = (probs[:].rearrange("p a u k -> p (a u k)")[:, a:a + 2 * DFF].rearrange(
            "p (r f) -> p r f", f=DFF) for a in (NTILE * TOPK * C, NTILE * TOPK * C + 2 * DFF))
        slot_rows = [sb(f"slot_rows{j}", [P, ROW]) for j in range(4)]
        slot_xt = sb("slot_xt", [P, 2, P])
        slot_y = [sb(f"slot_y{j}", [P, C]) for j in range(4)]
        o_rows = sb("o_rows", [P, 2, SEQ])
        rden = sb("rden", [P, TILES, QUADS])

        rank = sb("rank", [P, EXPERTS])
        top1 = sb("top1", [P, NTILE])
        top2 = sb("top2", [P, NTILE])
        best = sb("best", [P, NTILE])
        gap_exp = sb("gap_exp", [P, NTILE])
        gate1 = sb("gate1", [P, NTILE])
        gate2 = sb("gate2", [P, NTILE])
        n_slots = sb("n_slots", [P, EXPERTS])
        ends_a = sb("ends_a", [P, EXPERTS])
        ends_b = sb("ends_b", [P, EXPERTS])
        place = sb("place", [P, NTILE])
        places = sb("places", [P, TOPK, NTILE], I32)
        row_ids = sb("row_ids", [P, TOPK, NTILE], I32)
        expert_at = sb("expert_at", [P, SLOTS], I32)
        empty_row = sb("empty_row", [P, ROW])

        consts_dma = sem("consts_dma")
        x_loaded = sem("x_loaded")
        zeroed = sem("zeroed")
        pool_consts = sem("pool_consts")
        w_rows_ready = sem("w_rows_ready")
        decay_ready = sem("decay_ready")
        wdist_log = sem("wdist_log")
        wdist_ready = sem("wdist_ready")
        stats_ready = sem("stats_ready")
        var_ready = sem("var_ready")
        rstd_ready = sem("rstd_ready")
        xn_ready = sem("xn_ready")
        misc_full = sem("misc_full")
        misc_free = sem("misc_free")
        hi_ready = sem("hi_ready")
        k_loaded = sem("k_loaded")
        p1_full = sem("p1_full")
        p1_free = sem("p1_free")
        max_hi = sem("max_hi")
        max_ready = sem("max_ready")
        p2_full = sem("p2_full")
        exp_ready = sem("exp_ready")
        pool_probs = sem("pool_probs")
        dve_probs = sem("dve_probs")
        pv_full = sem("pv_full")
        o_ready = sem("o_ready")
        den_ready = sem("den_ready")
        xt_stored = [sem(f"xt_stored{r}") for r in range(2)]
        gates_step = sem("gates_step")
        gates_ready = sem("gates_ready")
        out_stored = sem("out_stored")
        experts_dma = sem("experts_dma")
        start_xt_full = sem("start_xt_full")
        start_xt_ready = sem("start_xt_ready")
        xt_loaded = sem("xt_loaded")
        logits_full = sem("logits_full")
        logits_ready = sem("logits_ready")
        filled = sem("filled")
        counts_full = sem("counts_full")
        rows_ready = sem("rows_ready")
        rows_sent = sem("rows_sent")
        slot_table = sem("slot_table")
        rows_loaded = [sem(f"rows_loaded{j}") for j in range(4)]
        slot_xt_full = sem("slot_xt_full")
        slot_xt_ready = sem("slot_xt_ready")
        up_full = sem("up_full")
        hidden_ready = sem("hidden_ready")
        turned_full = sem("turned_full")
        turned_ready = sem("turned_ready")
        down_full = sem("down_full")
        y_ready = sem("y_ready")
        y_sent = [sem(f"y_sent{j}") for j in range(4)]
        picked_loaded = [sem(f"picked_loaded{b}") for b in range(BATCH)]
        summed = sem("summed")
        attention_done = sem("attention_done")
        ident_ready = sem("ident_ready")
        row_masks = sem("row_masks")
        row_masks_step = sem("row_masks_step")
        gap_ready = sem("gap_ready")
        dve_init = sem("dve_init")
        act_init = sem("act_init")


        def unit_heads(w):
            return range(QUADS) if w == 4 else range(2 * (w % 2), 2 * (w % 2) + 2)

        def apply_decay(eng, at, w):
            heads = unit_heads(w)
            unit = probs[:, at.ring(2), w, :].rearrange("p (h k) -> p h k", h=len(heads))
            weights = wdist[:, at.g * QUADS + heads[0]:at.g * QUADS + heads[-1] + 1, :]
            parts = [(0, 384), (384, 512)] if w in (2, 3) else [(0, 1024 // len(heads))]
            for a, b in parts:
                last = eng.tensor_tensor(unit[:, :, a:b], unit[:, :, a:b], weights[:, :, 0:b - a], ALU.mult)
            return last

        N_POOL_CONSTS = 4
        with nc.Block() as block:
            @block.sync
            def _(sp):
                def x_rows(b):
                    return x_in[b].rearrange("(t p) c -> p t c", p=P)

                sp.dma_start(x_all[:, 0:TILES, :], x_rows(0)).then_inc(x_loaded, 16)
                sp.dma_start(w_qkv[:], w_attn).then_inc(consts_dma, 16)
                sp.dma_start(wr[:], wrt).then_inc(consts_dma, 16)
                sp.dma_start(decay_in[:], decay_raw.rearrange("(a h) -> a h", a=1).broadcast_to([P, HEADS])
                             ).then_inc(consts_dma, 16)
                sp.dma_start(wo[:], w_proj).then_inc(consts_dma, 16)
                sp.dma_start(x_all[:, TILES:, :], x_in[1:].rearrange("b (t p) c -> p (b t) c", p=P)
                             ).then_inc(x_loaded, 16)
                sp.wait_ge(slot_table, 2)
                sp.dma_start(rows_dram.rearrange("(s p) c -> p s c", p=P),
                             empty_row[:].rearrange("p (s c) -> p s c", s=1).broadcast_to([P, SLOTS, ROW])
                             ).then_inc(filled, 16)
                for n, b in enumerate(START_ORDER[:-2]):
                    sp.wait_ge(start_xt_ready, n + 1)
                    sp.dma_start(xt_dram[b - 2], xt[:, b % 2, :]).then_inc(xt_stored[b % 2], 16)
                sp.wait_ge(zeroed, 4)

                def k_step(at):
                    sp.wait_ge(misc_free, at.misc("K", 1))
                    for quad in range(QUADS):
                        rows = slice(quad * QROWS, (quad + 1) * QROWS)
                        sp.dma_start(k_heads[at.ring(4)][rows, quad, :].bitcast(F32),
                                     k_rows[rows, at.ring(2), :].bitcast(F32)).then_inc(k_loaded, 16)

                def xt_step(at):
                    for stored in xt_stored:
                        sp.wait_ge(stored, 16 * (BATCH // 2 - 1))
                    sp.wait_ge(misc_free, at.misc_before("K", GROUPS + 1, 1))
                    sp.dma_start(xt[:, at.parity, :], xt_dram[bass.ds(at.batches(1, -2), 1)].rearrange("b p s -> p (b s)")
                                 ).then_inc(xt_loaded, 16)

                run_slots(sp, {"K": k_step, "XT": xt_step})

                sp.wait_ge(pool_probs, len(POOL_UNITS) * NGROUP)
                sp.wait_ge(dve_probs, NGROUP)
                sp.dma_start(w1, w1t).then_inc(experts_dma, 16)
                sp.dma_start(w2.rearrange("p (f c) -> p f c", c=C), w2t.rearrange("e (f p) c -> p (e f) c", p=P)
                             ).then_inc(experts_dma, 16)

                def load_rows(i, j):
                    sp.dma_start(slot_rows[j][:], rows_dram[bass.ds(i * (4 * P) + j * P, P), :]
                                 ).then_inc(rows_loaded[j], 16)

                sp.wait_ge(rows_sent, 16 * NTILE * TOPK)
                for j in range(4):
                    load_rows(0, j)
                with sp.Fori(1, SLOTS // 4) as i:
                    for j in range(4):
                        sp.wait_ge(y_sent[j], i * 16)
                        load_rows(i, j)

                for j in range(4):
                    sp.wait_ge(y_sent[j], 16 * (SLOTS // 4))
                for b in range(BATCH):
                    sp.dma_start(picked[:, b * TILES:(b + 1) * TILES].rearrange("p t k c -> p t (k c)"),
                                 picked_dram.rearrange("(b t p k) c -> b p t (k c)", b=BATCH, t=TILES, k=TOPK)[b]
                                 ).then_inc(picked_loaded[b], 16)
                for b in range(BATCH):
                    sp.wait_ge(summed, 2 * b + 2)
                    sp.dma_start(out[b].rearrange("(t p) c -> p t c", p=P),
                                 x_all[:, b * TILES:(b + 1) * TILES, :]).then_inc(out_stored, 16)
                sp.wait_ge(out_stored, 16 * BATCH)
                sp.wait_ge(xt_loaded, 16 * (BATCH - 2))

            @block.gpsimd
            def _(pool):
                nc.gpsimd.memset(ident[:], 1.0).then_inc(pool_consts, 1)
                nc.gpsimd.memset(mask_q[:], 0.0).then_inc(pool_consts, 1)
                nc.gpsimd.memset(mask_k[:], 0.0).then_inc(pool_consts, 1)
                nc.gpsimd.memset(minus_half[:], -0.5).then_inc(pool_consts, 1)
                nc.gpsimd.memset(ones[:], 1.0).then_inc(pool_consts, 1)
                nc.gpsimd.memset(empty_row[:], 0.0).then_inc(slot_table, 1)
                pool.wait_ge(slot_table, 1)
                nc.gpsimd.iota(empty_row[:, 0:1].bitcast(I32), pattern=[[0, 1]], base=NOWHERE, channel_multiplier=1
                               ).then_inc(slot_table, 1)
                pool.wait_ge(pool_consts, 5)
                nc.gpsimd.affine_select(out=ident[:], in_=ident[:], compare_op=ALU.is_equal, fill=0.0, base=0,
                                        pattern=[[-1, P]], channel_multiplier=1).then_inc(ident_ready, 1)
                nc.gpsimd.affine_select(out=mask_q[:], in_=mask_q[:], compare_op=ALU.is_ge, fill=NEG, base=0,
                                        pattern=[[-1, P]], channel_multiplier=1).then_inc(ident_ready, 1)
                nc.gpsimd.affine_select(out=mask_k[:], in_=mask_k[:], compare_op=ALU.is_ge, fill=NEG, base=0,
                                        pattern=[[1, P]], channel_multiplier=-1).then_inc(ident_ready, 1)
                nc.gpsimd.iota(dist[:], pattern=[[1, SEQ]], base=0, channel_multiplier=-1,
                               allow_small_or_imprecise_dtypes=True).then_inc(ident_ready, 1)
                nc.gpsimd.iota(rank[:], pattern=[[-1, EXPERTS]], base=EXPERTS, channel_multiplier=0,
                               allow_small_or_imprecise_dtypes=True).then_inc(ident_ready, 1)
                pool.wait_ge(ident_ready, 1)
                nc.gpsimd.tensor_copy(ident_bf[:], ident[:]).then_inc(ident_ready, 1)
                nc.gpsimd.affine_select(out=before[:], in_=ones[:], compare_op=ALU.is_ge, fill=0.0, base=-1,
                                        pattern=[[1, P]], channel_multiplier=-1).then_inc(ident_ready, 1)
                nc.gpsimd.iota(slot_no[:], pattern=[[1, SLOTS]], base=0, channel_multiplier=0,
                               allow_small_or_imprecise_dtypes=True).then_inc(slot_table, 1)
                for k in range(TOPK):
                    nc.gpsimd.iota(row_ids[:, k, :], pattern=[[TOPK * P, NTILE]], base=k, channel_multiplier=TOPK
                                   ).then_inc(slot_table, 1)
                for t in k_heads:
                    nc.gpsimd.memset(t[:].bitcast(F32), 0.0).then_inc(zeroed, 1)

                pool.wait_ge(var_ready, 3)
                nc.gpsimd.tensor_tensor(rstd[:], var_eps[:], minus_half[:], ALU.pow).then_inc(rstd_ready, 1)

                def send_rows(pick):
                    pool.wait_ge(rows_ready, pick + 1)
                    for t in range(NTILE):
                        nc.gpsimd.indirect_dma_start(
                            out=rows_dram, out_offset=bass.IndirectOffsetOnAxis(
                                ap=places[:, pick, t:t + 1].bitcast(U32), axis=0),
                            in_=xn_all[:, t, :], in_offset=None).then_inc(rows_sent, 16)

                pool.wait_ge(filled, 16)
                send_rows(0)
                send_rows(1)

                def p2_step(at, w):
                    if w not in POOL_UNITS:
                        return
                    if not at.looped and at.c < GROUPS:
                        pool.wait_ge(wdist_ready, at.c + 1)
                    pool.wait_ge(exp_ready, at.groups(P2_UNITS, w + 1))
                    apply_decay(nc.gpsimd, at, w).then_inc(pool_probs, 1)

                run_slots(pool, {"P2": p2_step})

                def slot(i, j):
                    s = i * 4 + j
                    pool.wait_ge(y_ready, s + 1)
                    nc.gpsimd.nop(nofuse=True)
                    nc.gpsimd.indirect_dma_start(
                        out=picked_dram, out_offset=bass.IndirectOffsetOnAxis(
                            ap=slot_rows[j][:, 0:1].bitcast(U32), axis=0),
                        in_=slot_y[j][:], in_offset=None, bounds_check=last_row, oob_is_err=False
                    ).then_inc(y_sent[j], 16)

                last_row = nc.gpsimd.to_reg(BATCH * SEQ * TOPK - 1)
                with pool.Fori(0, SLOTS // 4) as i:
                    for j in range(4):
                        slot(i, j)

            @block.scalar
            def _(act):
                act.wait_ge(dve_init, 2)
                nc.scalar.activation(dec_exp[:], dec_abs[:], ACT.Exp, scale=-1.0).then_inc(act_init, 1)
                act.wait_ge(act_init, 1)
                nc.scalar.activation(dec_log[:], dec_exp[:], ACT.Ln, bias=1.0).then_inc(act_init, 1)
                act.wait_ge(dve_init, 3)
                nc.scalar.activation(log_dist[:], dist[:], ACT.Ln, bias=1.0).then_inc(act_init, 1)
                act.wait_ge(act_init, 3)
                act.wait_ge(row_masks, 2)

                for n, b in enumerate(START_ORDER):
                    act.wait_ge(start_xt_full, n + 1)
                    if n >= 2:
                        act.wait_ge(xt_stored[b % 2], 16 * (n // 2))
                    nc.scalar.activation(xt[:, b % 2, :], ps1[:, n % 2], ACT.Copy).then_inc(start_xt_ready, 1)
                act.wait_ge(logits_full, 1)
                nc.scalar.activation(logits[:], psM[:, 0:NTILE * EXPERTS], ACT.Copy).then_inc(logits_ready, 1)
                act.wait_ge(gates_step, GAP_STEP)
                nc.scalar.activation(gap_exp[:], gap_exp[:], ACT.Exp).then_inc(gap_ready, 1)

                def hi_step(kind, rows, number):
                    def step(at):
                        act.wait_ge(misc_full, at.misc(kind, 1))
                        nc.scalar.activation(hi_part[:].bitcast(F32R), psM[:], ACT.Copy,
                                             scale=rows[:, 0:1]).then_inc(hi_ready, 1)
                    return step

                def decay_weights(g):
                    act.wait_ge(decay_ready, 1)
                    for h in range(g * QUADS, (g + 1) * QUADS):
                        last = nc.scalar.activation(wdist[:, h, :], log_dist[:], ACT.Ln, bias=1.0,
                                                    scale=decay[:, h:h + 1])
                    last.then_inc(wdist_log, 1)
                    act.wait_ge(wdist_log, g + 1)
                    w = wdist[:, g * QUADS:(g + 1) * QUADS, :]
                    nc.scalar.activation(w, w, ACT.Exp, scale=-1.0).then_inc(wdist_ready, 1)

                def k_step(at):
                    hi_step("K", lo_row_k, 2)(at)
                    if not at.looped and at.c in (1, 2):
                        decay_weights(2 * at.c - 2)
                        decay_weights(2 * at.c - 1)

                def v_step(at):
                    act.wait_ge(misc_full, at.misc("V", 1))
                    nc.scalar.activation(values[:, at.parity, :, :, 0:HD],
                                         psM[:].rearrange("p (t h d) -> p t h d", t=TILES, h=HEADS),
                                         ACT.Copy).then_inc(misc_free, 1)

                def p2_step(at, w):
                    act.wait_ge(p2_full, at.groups(P2_UNITS, w + 1))
                    nc.scalar.activation(probs[:, at.ring(2), w, :],
                                         ps2[:, (at.c * P2_UNITS + w) % 2].rearrange("p a b -> p (a b)"),
                                         ACT.Exp).then_inc(exp_ready, 1)

                def pv_step(at, chunk):
                    if chunk == 3:
                        act.wait_ge(pv_full, at.groups(1, 1))
                        nc.scalar.activation(o_rows[:, at.ring(2), :], psO[:], ACT.Copy).then_inc(o_ready, 1)

                def yt_step(at):
                    act.wait_ge(misc_full, at.misc("YT", 1))
                    nc.scalar.activation(yt[:], psM[:], ACT.Copy).then_inc(misc_free, 1)

                run_slots(act, {"Q": hi_step("Q", lo_row_q, 1), "K": k_step,
                                "V": v_step, "P2": p2_step, "PV": pv_step, "YT": yt_step})

                def slot(i, j):
                    s = i * 4 + j
                    act.wait_ge(slot_xt_full, s + 1)
                    nc.scalar.activation(slot_xt[:, j % 2], psM[:, 0:P], ACT.Copy).then_inc(slot_xt_ready, 1)
                    act.wait_ge(up_full, s + 1)
                    nc.scalar.activation(hidden[:, j % 2], ps1[:, j % 2], ACT.Silu).then_inc(hidden_ready, 1)

                with act.Fori(0, SLOTS // 4) as i:
                    for j in range(4):
                        slot(i, j)

            @block.vector
            def _(dve):
                nc.vector.memset(values[:], 0.0).then_inc(dve_init, 1)
                dve.wait_ge(consts_dma, 16 * 4)
                nc.vector.tensor_scalar(dec_neg[:], decay_in[:], -1.0, None, ALU.mult).then_inc(row_masks_step, 1)
                dve.wait_ge(row_masks_step, 1)
                nc.vector.tensor_tensor(dec_abs[:], decay_in[:], dec_neg[:], ALU.max).then_inc(dve_init, 1)
                dve.wait_ge(ident_ready, 6)
                nc.vector.tensor_scalar(dist[:], dist[:], 0.0, None, ALU.max).then_inc(dve_init, 1)
                cols = ident[:].rearrange("p (q r) -> p q r", q=QUADS)
                for t, a, b in ((lo_row_q, ROW_LO, ROW_HI2), (lo_row_k, ROW_HI2, QROWS), (one_row_k, 0, 2)):
                    nc.vector.tensor_reduce(t[:], cols[:, :, a:b], AX.XY, ALU.add).then_inc(row_masks, 1)
                nc.vector.memset(wq_rows[:], 0.0).then_inc(row_masks_step, 1)
                nc.vector.memset(wk_rows[:], 0.0).then_inc(row_masks_step, 1)
                nc.vector.memset(max_cols[:], 0.0).then_inc(row_masks_step, 1)
                dve.wait_ge(dve_init, 1)
                nc.vector.memset(values[:, :, :, :, HD:HD + 1], 1.0).then_inc(row_masks_step, 1)
                dve.wait_ge(row_masks_step, 5)
                for first in (ROW_HI, ROW_LO, ROW_HI2):
                    for t, w, scale in ((wq_rows, 0, SCALE), (wk_rows, C, 1.0)):
                        nc.vector.tensor_scalar(
                            t[:].rearrange("p g (q r) -> p (g q) r", q=QUADS)[:, :, first:first + HD],
                            w_qkv[:, w:w + C].rearrange("p (h d) -> p h d", h=HEADS),
                            scale, None, ALU.mult).then_inc(w_rows_ready, 1)

                dve.wait_ge(act_init, 2)
                nc.vector.scalar_tensor_tensor(out=decay[:], in0=decay_in[:], scalar=0.0, in1=dec_log[:],
                                               op0=ALU.max, op1=ALU.add).then_inc(decay_ready, 1)

                v = nc.vector
                dve.wait_ge(x_loaded, 32)
                for t in range(NTILE):
                    last = v.bn_stats(stats[:, t, :], x_all[:, t, :])
                last.then_inc(stats_ready, 1)
                dve.wait_ge(stats_ready, 1)
                even, odd = stats[:, :, 0:3], stats[:, :, 3:6]
                v.tensor_tensor(mean[:], even[:, :, 1], odd[:, :, 1], ALU.add)
                v.tensor_tensor(between[:], even[:, :, 1], odd[:, :, 1], ALU.subtract)
                v.tensor_tensor(var_eps[:], even[:, :, 2], odd[:, :, 2], ALU.add).then_inc(var_ready, 1)
                dve.wait_ge(var_ready, 1)
                v.tensor_scalar(mean[:], mean[:], 0.5, None, ALU.mult)
                v.tensor_tensor(between[:], between[:], between[:], ALU.mult)
                v.tensor_scalar(var_eps[:], var_eps[:], 1.0 / C, EPS, ALU.mult, ALU.add).then_inc(var_ready, 1)
                dve.wait_ge(var_ready, 2)
                v.scalar_tensor_tensor(out=var_eps[:], in0=between[:], scalar=0.25, in1=var_eps[:], op0=ALU.mult,
                                       op1=ALU.add).then_inc(var_ready, 1)
                dve.wait_ge(rstd_ready, 1)
                for b in START_ORDER:
                    for t in range(b * TILES, (b + 1) * TILES):
                        last = v.tensor_scalar(xn_all[:, t, 2:], x_all[:, t, :], mean[:, t:t + 1],
                                               rstd[:, t:t + 1], ALU.subtract, ALU.mult)
                    last.then_inc(xn_ready, 1)

                done = [0]

                def step(instruction):
                    done[0] += 1
                    instruction.then_inc(gates_step, 1)
                    dve.wait_ge(gates_step, done[0])

                lg = logits[:].rearrange("p (t e) -> p t e", e=EXPERTS)

                def wide(t):
                    return t[:].rearrange("p (t a) -> p t a", a=1).broadcast_to([P, NTILE, EXPERTS])

                ranks = rank[:].rearrange("p (a e) -> p a e", a=1).broadcast_to([P, NTILE, EXPERTS])
                dve.wait_ge(logits_ready, 1)
                dve.wait_ge(ident_ready, 7)

                def first_of_best(src, top, pick):
                    step(v.tensor_reduce(top[:], src, AX.X, ALU.max))
                    step(v.tensor_tensor(pick[:], src, wide(top), ALU.is_equal))
                    step(v.tensor_tensor(pick[:], pick[:], ranks, ALU.mult))
                    step(v.tensor_reduce(best[:], pick[:], AX.X, ALU.max))
                    step(v.tensor_tensor(pick[:], pick[:], wide(best), ALU.is_equal))

                first_of_best(lg, top1, pick1)
                step(v.scalar_tensor_tensor(out=masked[:], in0=pick1[:], scalar=NEG, in1=lg,
                                            op0=ALU.mult, op1=ALU.add))
                first_of_best(masked[:], top2, pick2)
                step(v.tensor_tensor(masked[:], pick1[:], pick2[:], ALU.add))
                assert done[0] == PICKS_STEP
                step(v.tensor_tensor(gap_exp[:], top2[:], top1[:], ALU.subtract))
                assert done[0] == GAP_STEP
                dve.wait_ge(gap_ready, 1)
                step(v.tensor_scalar(gate1[:], gap_exp[:], 1.0, None, ALU.add))
                step(v.reciprocal(gate1[:], gate1[:]))
                step(v.tensor_tensor(gate2[:], gate1[:], gap_exp[:], ALU.mult))

                dve.wait_ge(counts_full, 1)
                within = psO[:, 0:256].rearrange("p (t e) -> p t e", e=EXPERTS)
                totals = psO[:, 256:512].rearrange("p (t e) -> p t e", e=EXPERTS)

                def running_sums(a, b, n):
                    d = 1
                    while d < n:
                        v.tensor_copy(b[:, 0:d], a[:, 0:d])
                        step(v.tensor_tensor(b[:, d:n], a[:, d:n], a[:, 0:n - d], ALU.add))
                        a, b = b, a
                        d *= 2
                    return a, b

                step(v.tensor_copy(sums_a[:], totals))
                sums, spare = running_sums(sums_a, sums_b, NTILE)
                step(v.tensor_scalar(n_slots[:], sums[:, NTILE - 1, :], 1.0 / P, (P - 1.0) / P - (P - 1.0) / (2 * P),
                                     ALU.mult, ALU.add))
                step(v.tensor_scalar(n_slots[:], n_slots[:], TWO23, None, ALU.add))
                step(v.tensor_scalar(n_slots[:], n_slots[:], TWO23, None, ALU.subtract))
                step(v.tensor_copy(ends_a[:], n_slots[:]))
                ends, starts = running_sums(ends_a, ends_b, EXPERTS)
                step(v.tensor_tensor(starts[:], ends[:], n_slots[:], ALU.subtract))
                step(v.tensor_scalar(starts[:], starts[:], float(P), None, ALU.mult))
                step(v.tensor_tensor(spare[:], sums[:], totals, ALU.subtract))
                step(v.tensor_tensor(spare[:], within, spare[:], ALU.add))
                step(v.tensor_tensor(spare[:], spare[:],
                                     starts[:].rearrange("p (a e) -> p a e", a=1).broadcast_to([P, NTILE, EXPERTS]),
                                     ALU.add))
                for k, pick in enumerate((pick1, pick2)):
                    step(v.tensor_tensor(pick[:], pick[:], spare[:], ALU.mult))
                    step(v.tensor_reduce(place[:], pick[:], AX.X, ALU.add))
                    step(v.tensor_copy(places[:, k, :], place[:]))

                def set_rows(k, gate):
                    dve.wait_ge(slot_table, 5)
                    v.tensor_copy(xn_all[:, :, 0].bitcast(I32), row_ids[:, k, :])
                    v.tensor_copy(xn_all[:, :, 1], gate[:]).then_inc(rows_ready, 1)

                set_rows(0, gate1)

                def spread(t, axis, n):
                    return t.rearrange("p (a b) -> p a b", **{axis: 1}).broadcast_to([P, SLOTS, EXPERTS])

                step(v.tensor_tensor(past[:], spread(slot_no[:], "b", SLOTS), spread(ends[:], "a", EXPERTS), ALU.is_ge))
                step(v.tensor_reduce(slot_expert[:], past[:], AX.X, ALU.add))
                step(v.tensor_scalar(slot_expert[:], slot_expert[:], EXPERTS - 1.0, float(DFF), ALU.min, ALU.mult))
                v.tensor_copy(expert_at[:], slot_expert[:]).then_inc(slot_table, 1)

                def q_step(at):
                    dve.wait_ge(hi_ready, at.groups(2, 1))
                    nc.vector.tensor_tensor(q_rows[:, at.ring(4), :], psM[:], hi_part[:],
                                            ALU.subtract).then_inc(misc_free, 1)

                def k_step(at):
                    dve.wait_ge(hi_ready, at.groups(2, 2))
                    nc.vector.scalar_tensor_tensor(out=k_rows[:, at.ring(2), :], in0=psM[:],
                                                   scalar=one_row_k[:, 0:1], in1=hi_part[:], op0=ALU.add,
                                                   op1=ALU.subtract).then_inc(misc_free, 1)

                def p1_step(at, u0, u1):
                    for u in range(u0, u1):
                        bank = ps1[:, u % 2]
                        r = at.ring(2)
                        dve.wait_ge(p1_full, at.groups(P1_UNITS, u + 1))
                        pair, v = u // 5, u % 5
                        if v < 2:
                            todo = [(bank[:, 0:512], neg_max[:, r, 3, 2 * pair + v:2 * pair + v + 1])]
                        elif v < 4:
                            q = 2 * pair + v - 2
                            todo = [(bank[:, 0:384], neg_max[:, r, 2, q:q + 1]),
                                    (bank[:, 384:512], neg_max[:, r, 0, q:q + 1])]
                        else:
                            todo = [(bank.rearrange("p (h k) -> p h k", h=2),
                                     neg_max[:, r, 1, 2 * pair:2 * pair + 2])]
                        for src, dst in todo:
                            last = nc.vector.tensor_reduce(dst, src, AX.X, ALU.max, negate=True)
                        last.then_inc(p1_free, 1)

                def send_second():
                    dve.wait_ge(rows_sent, 16 * NTILE)
                    set_rows(1, gate2)

                def hl_step(at):
                    if not at.looped and at.c == SECOND_PICK_SLOT - 1:
                        send_second()
                    dve.wait_ge(p1_free, at.groups(P1_UNITS, P1_UNITS))
                    r = at.ring(2)
                    hi = max_cols[:, r, :, :, 0]
                    nc.vector.tensor_copy(hi.bitcast(F32R), neg_max[:, r]).then_inc(max_hi, 1)
                    dve.wait_ge(max_hi, at.groups(1, 1))
                    nc.vector.tensor_tensor(max_cols[:, r, :, :, 1], neg_max[:, r], hi,
                                            ALU.subtract).then_inc(max_ready, 1)

                def mt_step(at):
                    dve.wait_ge(misc_full, at.misc("MT", 1))
                    q = q_rows[:, at.ring(4), :]
                    nc.vector.tensor_tensor(q, psM[:], q.bitcast(F32), ALU.add).then_inc(misc_free, 1)

                def p2_step(at, w):
                    if w in DVE_UNITS:
                        if not at.looped and at.c < GROUPS:
                            dve.wait_ge(wdist_ready, at.c + 1)
                        dve.wait_ge(exp_ready, at.groups(P2_UNITS, 5))
                        apply_decay(nc.vector, at, 4).then_inc(dve_probs, 1)

                def nt_step(at):
                    dve.wait_ge(misc_full, at.misc("NT", 1))
                    o = psM[:].rearrange("p (t q r) -> p t q r", t=TILES, q=QUADS)
                    nc.vector.reciprocal(rden[:], o[:, :, :, HD]).then_inc(den_ready, 1)
                    dve.wait_ge(den_ready, at.groups(1, 1))
                    c0 = at.g * QUADS * HD
                    nc.vector.tensor_tensor(
                        y[:, at.parity, :, c0:c0 + QUADS * HD].rearrange("p t (q d) -> p t q d", q=QUADS),
                        o[:, :, :, 0:HD],
                        rden[:].rearrange("p t (q a) -> p t q a", a=1).broadcast_to([P, TILES, QUADS, HD]),
                        ALU.mult).then_inc(misc_free, 1)

                def pj_step(at):
                    dve.wait_ge(misc_full, at.misc("PJ", 1))
                    x = x_all[:, bass.ds(at.batches(TILES), TILES), :]
                    nc.vector.tensor_tensor(x, psM[:].rearrange("p (t c) -> p t c", t=TILES), x,
                                            ALU.add).then_inc(misc_free, 1)

                run_slots(dve, {"Q": q_step, "K": k_step,
                                "P1": p1_step, "HL": hl_step, "MT": mt_step, "P2": p2_step, "NT": nt_step,
                                "PJ": pj_step})

                def slot(i, j):
                    s = i * 4 + j
                    dve.wait_ge(turned_full, s + 1)
                    v.tensor_copy(hidden_t[:, j % 2], ps2[:, 0, j % 2]).then_inc(turned_ready, 1)
                    dve.wait_ge(down_full, s + 1)
                    v.tensor_scalar(slot_y[j][:], ps2[:, 1, j % 2, 0:C], slot_rows[j][:, 1:2], None,
                                    ALU.mult).then_inc(y_ready, 1)

                with dve.Fori(0, SLOTS // 4) as i:
                    for j in range(4):
                        slot(i, j)

                for b in range(BATCH):
                    x = x_all[:, b * TILES:(b + 1) * TILES, :]
                    dve.wait_ge(picked_loaded[b], 16)
                    for k in range(TOPK):
                        v.tensor_tensor(x, x, picked[:, b * TILES:(b + 1) * TILES, k, :], ALU.add).then_inc(summed, 1)
                        dve.wait_ge(summed, TOPK * b + k + 1)

            @block.tensor
            def _(pe):
                pe.wait_ge(ident_ready, 7)
                pe.wait_ge(w_rows_ready, 6)
                mm = nc.tensor.matmul

                def misc_use(at, kind):
                    if MISC[kind, at.c] or at.looped:
                        pe.wait_ge(misc_free, at.misc(kind))

                def transposes(src):
                    for t in range(TILES):
                        last = nc.tensor.transpose(psM[:, t * P:(t + 1) * P], src(t), ident[:])
                    last.then_inc(misc_full, 1)

                def start_logits(n):
                    b = START_ORDER[n]
                    pe.wait_ge(start_xt_ready, n + 1)
                    for t in range(TILES):
                        last = mm(psM[:, (b * TILES + t) * EXPERTS:(b * TILES + t + 1) * EXPERTS],
                                  xt[:, b % 2, t * P:(t + 1) * P], wr[:], start=True, stop=True)
                    return last

                for n, b in enumerate(START_ORDER):
                    pe.wait_ge(xn_ready, n + 1)
                    if n >= 2:
                        pe.wait_ge(start_xt_ready, n - 1)
                    for t in range(TILES):
                        last = nc.tensor.transpose(ps1[:, n % 2, t * P:(t + 1) * P], xn_all[:, b * TILES + t, 2:],
                                                   ident[:])
                    last.then_inc(start_xt_full, 1)
                    if n >= 1:
                        start_logits(n - 1)
                start_logits(BATCH - 1).then_inc(logits_full, 1)
                pe.wait_ge(gates_step, PICKS_STEP)
                picks = masked[:].rearrange("p t e -> p (t e)")
                mm(psO[:, 0:256], before[:], picks, start=True, stop=True)
                mm(psO[:, 256:512], ones[:], picks, start=True, stop=True).then_inc(counts_full, 1)

                def v_step(at):
                    misc_use(at, "V")
                    for t in range(TILES):
                        last = mm(psM[:, t * C:(t + 1) * C], xt[:, at.parity, t * P:(t + 1) * P],
                                  w_qkv[:, 2 * C:3 * C], start=True, stop=True)
                    last.then_inc(misc_full, 1)

                def rows_step(kind, w):
                    def step(at):
                        misc_use(at, kind)
                        if kind == "Q" and at.g == 0 and (at.looped or at.c >= 2 * GROUPS):
                            pe.wait_ge(xt_loaded, at.batches(16, -16))
                        mm(psM[:], w[:, at.g, :], xt[:, at.parity, :], start=True, stop=True).then_inc(misc_full, 1)
                    return step

                def p1_step(at, u0, u1):
                    q = q_rows[:, at.ring(4), :]
                    k = k_heads[at.ring(4)]

                    def scores(dst, tile, quad):
                        n = (tile + 1) * P
                        mm(dst[:, 0:n], q[:, tile * P:n], k[:, quad, 0:n], start=True, stop=False)
                        return mm(dst[:, n - P:n], ident_bf[:], mask_q[:], start=False, stop=True)

                    if u0 == 0:
                        pe.wait_ge(misc_free, at.misc("K", 1))
                        pe.wait_ge(k_loaded, at.groups(64, 64))
                    for u in range(u0, u1):
                        if at.looped or at.c * P1_UNITS + u >= 2:
                            pe.wait_ge(p1_free, at.groups(P1_UNITS, u - 1))
                        bank = ps1[:, u % 2]
                        pair, v = u // 5, u % 5
                        if v < 2:
                            last = scores(bank, 3, 2 * pair + v)
                        elif v < 4:
                            scores(bank[:, 0:384], 2, 2 * pair + v - 2)
                            last = scores(bank[:, 384:512], 0, 2 * pair + v - 2)
                        else:
                            scores(bank[:, 0:256], 1, 2 * pair)
                            last = scores(bank[:, 256:512], 1, 2 * pair + 1)
                        last.then_inc(p1_full, 1)

                def mt_step(at):
                    misc_use(at, "MT")
                    pe.wait_ge(max_ready, at.groups(1, 1))
                    transposes(lambda t: max_cols[:, at.ring(2), t].rearrange("p q r -> p (q r)"))

                def p2_step(at, w):
                    q = q_rows[:, at.ring(4), :]
                    k = k_heads[at.ring(4)]
                    if w == 0:
                        pe.wait_ge(misc_free, at.misc("MT", 1))
                    if at.looped or at.c * P2_UNITS + w >= 2:
                        pe.wait_ge(exp_ready, at.groups(P2_UNITS, w - 1))
                    pair = ps2[:, (at.c * P2_UNITS + w) % 2]

                    def scores(dst, tile, quad):
                        a = tile * P
                        mm(dst, k[:, quad, a:a + P], q[:, a:], start=True, stop=False)
                        return mm(dst[:, 0:P], ident_bf[:], mask_k[:], start=False, stop=True)

                    for s, quad in enumerate(unit_heads(w)):
                        if w < 2:
                            last = scores(pair[:, s, :], 0, quad)
                        elif w < 4:
                            scores(pair[:, s, 0:384], 1, quad)
                            last = scores(pair[:, s, 384:512], 3, quad)
                        else:
                            last = scores(pair[:, s // 2, s % 2 * 256:s % 2 * 256 + 256], 2, quad)
                    last.then_inc(p2_full, 1)

                def pv_step(at, chunk):
                    if chunk == 0 and (at.looped or at.c > 0):
                        pe.wait_ge(o_ready, at.groups(1))
                    if chunk == 3:
                        pe.wait_ge(dve_probs, at.groups(1, 1))
                    else:
                        pe.wait_ge(pool_probs, at.groups(4, 2 if chunk == 0 else 4))
                    tile = (0, 1, 3, 2)[chunk]
                    for quad in range(QUADS):
                        unit, a, n = {0: (quad // 2, quad % 2 * 512, 512), 1: (2 + quad // 2, quad % 2 * 512, 384),
                                      3: (2 + quad // 2, quad % 2 * 512 + 384, 128), 2: (4, quad * 256, 256)}[tile]
                        last = mm(psO[quad * QROWS:(quad + 1) * QROWS, tile * P:],
                                  values[:, at.parity, tile, at.g * QUADS + quad, :],
                                  probs[:, at.ring(2), unit, a:a + n], start=(chunk == 0), stop=(chunk == 3))
                    if chunk == 3:
                        last.then_inc(pv_full, 1)

                def nt_step(at):
                    misc_use(at, "NT")
                    pe.wait_ge(o_ready, at.groups(1, 1))
                    transposes(lambda t: o_rows[:, at.ring(2), t * P:(t + 1) * P])

                def yt_step(at):
                    misc_use(at, "YT")
                    transposes(lambda t: y[:, at.parity, t, :])

                def pj_step(at):
                    misc_use(at, "PJ")
                    for t in range(TILES):
                        last = mm(psM[:, t * C:(t + 1) * C], yt[:, t * P:(t + 1) * P], wo[:], start=True, stop=True)
                    last.then_inc(misc_full, 1)

                run_slots(pe, {"V": v_step, "Q": rows_step("Q", wq_rows),
                               "K": rows_step("K", wk_rows), "P1": p1_step, "MT": mt_step, "P2": p2_step,
                               "PV": pv_step, "NT": nt_step, "YT": yt_step, "PJ": pj_step})

                pe.wait_ge(experts_dma, 32)
                pe.wait_ge(slot_table, 6)
                pe.wait_ge(misc_free, len(MISC))
                pe.wait_ge(exp_ready, P2_ALL)
                pe.wait_ge(p1_free, P1_ALL)

                def positive(s, less):
                    return not isinstance(s, int) or s - less >= 0

                def turn_tokens(i, j):
                    s = i * 4 + j
                    pe.wait_ge(rows_loaded[j % 4], (i + j // 4) * 16 + 16)
                    if positive(s, 1):
                        pe.wait_ge(slot_xt_ready, s)
                    nc.tensor.transpose(psM[:, 0:P], slot_rows[j % 4][:, 2:], ident[:]).then_inc(slot_xt_full, 1)

                def up(i, j):
                    s = i * 4 + j
                    at = nc.tensor.value_load(expert_at[0:1, bass.ds(s, 1)], min_val=0, max_val=(EXPERTS - 1) * DFF)
                    pe.wait_ge(slot_xt_ready, s + 1)
                    if positive(s, 2):
                        pe.wait_ge(hidden_ready, s - 1)
                    mm(ps1[:, j % 2], slot_xt[:, j % 2], w1[:, bass.ds(at, DFF)], start=True, stop=True
                       ).then_inc(up_full, 1)
                    return at

                def turn_hidden(i, j):
                    s = i * 4 + j
                    pe.wait_ge(hidden_ready, s + 1)
                    if positive(s, 2):
                        pe.wait_ge(turned_ready, s - 1)
                    for f in range(FT):
                        last = nc.tensor.transpose(ps2[:, 0, j % 2, f * P:(f + 1) * P],
                                                   hidden[:, j % 2, f * P:(f + 1) * P], ident[:])
                    last.then_inc(turned_full, 1)

                def down(i, j, at):
                    s = i * 4 + j
                    pe.wait_ge(turned_ready, s + 1)
                    if positive(s, 2):
                        pe.wait_ge(y_ready, s - 1)
                    for f in range(FT):
                        last = mm(ps2[:, 1, j % 2, 0:C], hidden_t[:, j % 2, f * P:(f + 1) * P],
                                  w2[:, bass.ds(at + f * C, C)], start=(f == 0), stop=(f == FT - 1))
                    last.then_inc(down_full, 1)

                def four_slots(i, last):
                    for j in range(4):
                        more = not (last and j == 3)
                        if more:
                            turn_tokens(i, j + 1)
                        turn_hidden(i, j)
                        if more:
                            up(i, j + 1)
                        at = nc.tensor.value_load(expert_at[0:1, bass.ds(i * 4 + j, 1)], min_val=0,
                                                  max_val=(EXPERTS - 1) * DFF)
                        down(i, j, at)

                turn_tokens(0, 0)
                up(0, 0)
                four_slots(0, False)
                with pe.Fori(1, SLOTS // 4 - 1) as i:
                    four_slots(i, False)
                four_slots(SLOTS // 4 - 1, True)


def kernel(L0_attn_x, L0_attn_w_attn, L0_attn_w_proj, L0_attn_decay_raw, L0_ffn_W1, L0_ffn_W2, L0_ffn_Wr):
    import numpy as np
    import concourse.bacc as bacc
    from concourse.bass_utils import run_bass_kernel_spmd

    nc = bacc.Bacc("TRN2", target_bir_lowering=False, num_devices=1)
    arrays = {
        "x": np.asarray(L0_attn_x),
        "w_attn": np.asarray(L0_attn_w_attn),
        "w_proj": np.asarray(L0_attn_w_proj),
        "decay_raw": np.asarray(L0_attn_decay_raw),
        "w1t": np.asarray(L0_ffn_W1).transpose(2, 0, 1).reshape(C, EXPERTS * DFF),
        "w2t": np.asarray(L0_ffn_W2).transpose(0, 2, 1),
        "wrt": np.asarray(L0_ffn_Wr).T,
    }
    arrays = {k: np.ascontiguousarray(v) for k, v in arrays.items()}
    args = [nc.dram_tensor(k, v.shape, mybir.dt.from_np(v.dtype), kind="ExternalInput").ap() for k, v in arrays.items()]
    out = nc.dram_tensor("out", (BATCH, SEQ, C), F32, kind="ExternalOutput").ap()
    build(nc, *args, out)
    return run_bass_kernel_spmd(nc, [arrays], core_ids=[0]).results[0]["out"]
```

```python
from contextlib import ExitStack

import concourse.bass as bass
from concourse import mybir

F32 = mybir.dt.float32
F32R = mybir.dt.float32r
I32 = mybir.dt.int32
U32 = mybir.dt.uint32
BF16 = mybir.dt.bfloat16
ALU = mybir.AluOpType
ACT = mybir.ActivationFunctionType
AX = mybir.AxisListType

P = 128
BATCH, SEQ, C = 8, 512, 128
HEADS = 16
HD = C // HEADS
QUADS = 4
QROWS = P // QUADS
GROUPS = HEADS // QUADS
NGROUP = BATCH * GROUPS
TILES = SEQ // P
NTILE = BATCH * TILES
EXPERTS, DFF = 8, 512
FT = DFF // P
EPS = 1e-5
SCALE = float(HD) ** -0.5
NEG = -3.0e38
ROW_HI, ROW_LO, ROW_HI2 = 8, 16, 24

P1_UNITS = 10
P2_UNITS = 5
DVE_TILES, DVE_TILES_LAST, LAST_GROUPS = (3, 2), (1, 3, 2), 2
TILE_UNITS = {0: (0, 1), 1: (2, 3), 2: (4,), 3: (2, 3)}
TILE_COLS = {0: slice(0, 512), 1: slice(0, 384), 2: slice(0, 256), 3: slice(384, 512)}
DVE_BATCHES, POOL_BATCHES = (0, 1, 3, 4, 6, 7), (2, 5)
P1_ALL, P2_ALL = P1_UNITS * NGROUP, P2_UNITS * NGROUP
TOPK = 2
SECOND_PICK_SLOT = 3
SLOTS_USED = (BATCH * SEQ * TOPK + EXPERTS * (P - 1)) // P
SLOTS_UNROLL = 12
SLOT_LOOPS = -(-SLOTS_USED // SLOTS_UNROLL)
SLOTS = SLOT_LOOPS * SLOTS_UNROLL
RING = 6
ACT_UNROLL = 24
ROW = C + 2
TOKEN_ROW = 1 + ROW
NOWHERE = 1 << 20
NORM_PARTS = (slice(0, TILES), slice(TILES, NTILE))
PICKS_STEP, GAP_STEP = 12, 13
TWO23 = 8388608.0

LOOP_FIRST, LOOP_SLOTS, LOOP_TIMES = 5, 8, 3
LAST_SLOT = NGROUP + 5


def dve_tiles(at):
    return DVE_TILES_LAST if not at.looped and at.c >= NGROUP - LAST_GROUPS else DVE_TILES


def decay_done(at, tile):
    last_groups = 0 if dve_tiles(at) is DVE_TILES else at.c - (NGROUP - LAST_GROUPS)
    if tile in dve_tiles(at):
        return True, at.groups(len(DVE_TILES), 1 + dve_tiles(at).index(tile) + last_groups)
    return False, at.groups(4, (2, 4)[tile] - 2 * last_groups)


def slot_steps(n):
    steps = []

    def step(kind, index, limit, *more):
        if 0 <= index < limit:
            steps.append((kind, index - n, *more))

    def per_batch(kind, phase):
        if (n - phase) % GROUPS == 0:
            b = (n - phase) // GROUPS
            if 0 <= b < BATCH and b >= {"XT": 2, "QA": 1, "KA": 1}.get(kind, 0):
                steps.append((kind, b * GROUPS - n))

    step("HL", n - 1, NGROUP)
    step("P1", n, NGROUP, 0, 2)
    per_batch("V", 2)
    per_batch("YT", 8)
    step("DW", n - 3, NGROUP, (1, 3))
    step("P2", n - 2, NGROUP, 0)
    step("PV", n - 3, NGROUP, 0)
    step("K", n + 1, NGROUP)
    step("P1", n, NGROUP, 2, 4)
    step("DW", n - 3, NGROUP, (2,))
    step("P2", n - 2, NGROUP, 1)
    per_batch("KA", -2)
    per_batch("QA", -1)
    per_batch("PJ", 8)
    step("PV", n - 3, NGROUP, 1)
    step("P1", n, NGROUP, 4, 6)
    step("P2", n - 2, NGROUP, 2)
    step("Q", n + 1, NGROUP)
    step("PV", n - 3, NGROUP, 2)
    per_batch("XT", -3)
    step("P1", n, NGROUP, 6, 8)
    step("P2", n - 2, NGROUP, 3)
    step("MT", n - 1, NGROUP)
    step("PV", n - 3, NGROUP, 3)
    step("P1", n, NGROUP, 8, 10)
    step("NT", n - 4, NGROUP)
    step("P2", n - 2, NGROUP, 4)
    step("SC", n - SECOND_PICK_SLOT - 1, NTILE)
    if n == SECOND_PICK_SLOT:
        steps.append(("SR", 0))
    step("SL", n - SECOND_PICK_SLOT, NTILE)
    step("WL", n - NGROUP, GROUPS)
    return steps


PROLOGUE = [("KA", 0), ("QA", 0), ("K", 0), ("Q", 0)]
MISC_KINDS = ("QA", "KA", "V", "Q", "K", "MT", "NT", "YT", "PJ")




def misc_uses():
    uses = {}
    for kind, d in PROLOGUE:
        if kind in MISC_KINDS:
            uses[kind, d] = len(uses)
    for n in range(LAST_SLOT):
        for kind, d, *_ in slot_steps(n):
            if kind in MISC_KINDS:
                uses[kind, n + d] = len(uses)
    return uses


MISC = misc_uses()
MISC_PERIOD = MISC["MT", 8 + 8] - MISC["MT", 8]


class At:

    def __init__(self, i, c):
        if isinstance(i, int):
            self.i, self.c, self.looped = 0, LOOP_SLOTS * i + c, False
        else:
            self.i, self.c, self.looped = i, c, True

    def groups(self, per, more=0):
        k = per * self.c + more
        return self.i * (per * LOOP_SLOTS) + k if self.looped else k

    def batches(self, per, more=0):
        k = per * (self.c // GROUPS) + more
        return self.i * (per * LOOP_SLOTS // GROUPS) + k if self.looped else k

    def misc(self, kind, more=0):
        k = MISC[kind, self.c] + more
        return self.i * MISC_PERIOD + k if self.looped else k

    def misc_before(self, kind, groups, more=0):
        k = MISC[kind, self.c - groups] + more
        return self.i * MISC_PERIOD + k if self.looped else k

    @property
    def g(self):
        return self.c % GROUPS

    def ring(self, size):
        return self.c % size

    @property
    def parity(self):
        return self.c // GROUPS % 2


def run_prologue(steps):
    for kind, d in PROLOGUE:
        if kind in steps:
            steps[kind](At(0, d))


def run_slots(eng, steps):
    def slot(i, c, n):
        for kind, d, *more in slot_steps(n):
            if kind in steps:
                steps[kind](At(i, c + d), *more)

    for n in range(LOOP_FIRST):
        slot(0, n, n)
    with eng.Fori(0, LOOP_TIMES) as i:
        for c in range(LOOP_FIRST, LOOP_FIRST + LOOP_SLOTS):
            slot(i, c, c)
    done = LOOP_FIRST + LOOP_SLOTS * LOOP_TIMES
    for n in range(done, LAST_SLOT):
        slot(0, n, n)


def build(nc, x_in, w_attn, w_proj, decay_raw, w1t, w2t, wrt, out):
    with ExitStack() as ctx:
        def sb(name, shape, dt=F32):
            return ctx.enter_context(nc.sbuf_tensor(name, shape, dt))

        def sem(name):
            return ctx.enter_context(nc.semaphore(name))

        xt_dram = nc.dram_tensor("xt_dram", (BATCH - 2, P, SEQ), F32).ap()
        rows_dram = nc.dram_tensor("rows_dram", (SLOTS * P, ROW), F32).ap()
        picked_dram = nc.dram_tensor("picked_dram", (BATCH * SEQ * TOPK, C), F32).ap()

        ps1 = ctx.enter_context(nc.psum_tensor("ps1", [P, 2, 512], F32))
        ps2 = ctx.enter_context(nc.psum_tensor("ps2", [P, 2, 2, 512], F32))
        psO = ctx.enter_context(nc.psum_tensor("psO", [P, 512], F32))
        psM = ctx.enter_context(nc.psum_tensor("psM", [P, 512], F32))

        ident = sb("ident", [P, P])
        ident_bf = sb("ident_bf", [P, P], BF16)
        mask_k = sb("mask_k", [P, P], BF16)
        mask_q = sb("mask_q", [P, 2 * P], BF16)
        one_row_k = sb("one_row_k", [P, 1])
        minus_half = sb("minus_half", [P, NTILE])
        w_qkv = sb("w_qkv", [P, 3 * C])
        w_q = sb("w_q", [P, C])
        q_hi_to, q_lo_to, k_hi_to, k_lo_to = (sb(f"{name}_to", [P, GROUPS, P], F32R)
                                              for name in ("q_hi", "q_lo", "k_hi", "k_lo"))
        wo = sb("wo", [P, C])
        wr = sb("wr", [P, EXPERTS])
        decay = sb("decay", [P, HEADS])
        decay_in = sb("decay_in", [P, HEADS])
        dec_neg = sb("dec_neg", [P, HEADS])
        dec_abs = sb("dec_abs", [P, HEADS])
        dec_exp = sb("dec_exp", [P, HEADS])
        dec_log = sb("dec_log", [P, HEADS])
        wdist = sb("wdist", [P, HEADS, SEQ])
        w2 = wdist[:, HEADS // 2:, :].rearrange("p h s -> p (h s)")
        w1 = wdist[:, 0:HEADS // 2, :].rearrange("p h s -> p (h s)")
        x_all = sb("x_all", [P, NTILE, C])
        xn_all = sb("xn_all", [P, NTILE, TOKEN_ROW])
        mean = sb("mean", [P, NTILE])
        between = sb("between", [P, NTILE])
        var_eps = sb("var_eps", [P, NTILE])
        rstd = sb("rstd", [P, NTILE])
        xt = sb("xt", [P, 2, SEQ])
        values = sb("values", [P, 2, TILES, HEADS, QROWS])
        y = sb("y", [P, 2, TILES, C])
        yt = sb("yt", [P, SEQ])
        q_hi, q_lo, k_hi, k_lo = (sb(name, [P, SEQ], F32R) for name in ("q_hi", "q_lo", "k_hi", "k_lo"))
        q_rows = sb("q_rows", [P, 4, SEQ], F32R)
        k_rows = sb("k_rows", [P, 2, SEQ], F32R)
        k_heads = [sb(f"k_heads{r}", [P, QUADS, SEQ], F32R) for r in range(4)]
        neg_max = sb("neg_max", [P, 2, TILES, QUADS])
        max_cols = sb("max_cols", [P, 2, TILES, QUADS, QROWS])
        probs = sb("probs", [P, 2, P2_UNITS, 1024])
        start_used = [0]

        def early(*shape):
            n = 1
            for k in shape:
                n *= k
            a = start_used[0]
            start_used[0] += n
            part = probs[:].rearrange("p a u k -> p (a u k)")[:, a:a + n]
            return part.rearrange("p (a b) -> p a b", b=shape[1]) if len(shape) == 2 else part

        ones = early(P)
        before = early(P)
        stats = early(NTILE, 6)
        logits = early(NTILE * EXPERTS)
        dist = early(SEQ)
        log_dist = early(SEQ)
        masked, pick1, pick2 = early(NTILE, EXPERTS), early(NTILE, EXPERTS), early(NTILE, EXPERTS)
        sums_a, sums_b = early(NTILE, EXPERTS), early(NTILE, EXPERTS)
        slot_no = early(SLOTS)
        past = early(SLOTS, EXPERTS)
        slot_expert = early(SLOTS)
        empty_row = early(ROW)
        top1, top2, best, gap_exp, place = (early(NTILE) for _ in range(5))
        xt_early = early(BATCH - 2, SEQ)
        picked = probs[:].rearrange("p a u k -> p (a u k)")[:, 0:NTILE * TOPK * C].rearrange(
            "p (t k c) -> p t k c", k=TOPK, c=C)
        hidden, hidden_t = (probs[:].rearrange("p a u k -> p (a u k)")[:, a:a + 2 * DFF].rearrange(
            "p (r f) -> p r f", f=DFF) for a in (NTILE * TOPK * C, NTILE * TOPK * C + 2 * DFF))
        send_rows = [sb(f"send_rows{r}", [P, TOKEN_ROW]) for r in range(2)]
        slot_rows = [k_heads[0][:].bitcast(F32).rearrange("p q s -> p (q s)")[:, j * ROW:(j + 1) * ROW]
                     for j in range(RING)]
        slot_xt, slot_y8 = (values[:].rearrange("p a t h r -> p (a t h r)")[:, a:a + n * P].rearrange(
            "p (r c) -> p r c", c=P) for a, n in ((0, 2), (2 * P, RING)))
        slot_y = [slot_y8[:, j] for j in range(RING)]
        o_rows = sb("o_rows", [P, 2, SEQ])
        rden = sb("rden", [P, TILES, QUADS])

        rank = sb("rank", [P, EXPERTS])
        gate1 = sb("gate1", [P, NTILE])
        gate2 = sb("gate2", [P, NTILE])
        n_slots = sb("n_slots", [P, EXPERTS])
        ends_a = sb("ends_a", [P, EXPERTS])
        ends_b = sb("ends_b", [P, EXPERTS])
        places = sb("places", [P, TOPK, NTILE], I32)
        row_ids = sb("row_ids", [P, TOPK, NTILE], I32)
        expert_at = sb("expert_at", [P, SLOTS], I32)

        consts_dma = sem("consts_dma")
        first_x_loaded = sem("first_x_loaded")
        x_loaded = sem("x_loaded")
        zeroed = sem("zeroed")
        pool_consts = sem("pool_consts")
        w_rows_ready = sem("w_rows_ready")
        decay_ready = sem("decay_ready")
        wdist_log = sem("wdist_log")
        wdist_ready = sem("wdist_ready")
        wdist_causal = sem("wdist_causal")
        stats_ready = sem("stats_ready")
        var_ready = sem("var_ready")
        rstd_ready = sem("rstd_ready")
        xn_ready = sem("xn_ready")
        misc_full = sem("misc_full")
        misc_free = sem("misc_free")
        hi_ready = sem("hi_ready")
        k_loaded = sem("k_loaded")
        p1_full = sem("p1_full")
        p1_free = sem("p1_free")
        max_hi = sem("max_hi")
        max_ready = sem("max_ready")
        p2_full = sem("p2_full")
        exp_ready = sem("exp_ready")
        pool_probs = sem("pool_probs")
        dve_probs = sem("dve_probs")
        pv_full = sem("pv_full")
        o_ready = sem("o_ready")
        den_ready = sem("den_ready")
        xt_stored = sem("xt_stored")
        gates_step = sem("gates_step")
        out_stored = sem("out_stored")
        w1_dma = sem("w1_dma")
        w2_dma = sem("w2_dma")
        start_xt_full = sem("start_xt_full")
        start_xt_ready = sem("start_xt_ready")
        xt_loaded = sem("xt_loaded")
        logits_full = sem("logits_full")
        logits_ready = sem("logits_ready")
        filled = sem("filled")
        counts_full = sem("counts_full")
        rows_ready = sem("rows_ready")
        rows_sent = sem("rows_sent")
        send_loaded = [sem(f"send_loaded{r}") for r in range(2)]
        second_sent = [sem(f"second_sent{r}") for r in range(2)]
        slot_table = sem("slot_table")
        rows_loaded = [sem(f"rows_loaded{j}") for j in range(RING)]
        slot_xt_full = sem("slot_xt_full")
        slot_xt_ready = sem("slot_xt_ready")
        up_full = sem("up_full")
        hidden_ready = sem("hidden_ready")
        turned_full = sem("turned_full")
        turned_ready = sem("turned_ready")
        down_full = sem("down_full")
        y_ready = sem("y_ready")
        y_sent = [sem(f"y_sent{j}") for j in range(RING)]
        picked_loaded = [sem(f"picked_loaded{b}") for b in range(BATCH)]
        dve_summed = sem("dve_summed")
        pool_summed = sem("pool_summed")
        ident_ready = sem("ident_ready")
        row_masks = sem("row_masks")
        row_masks_step = sem("row_masks_step")
        gap_ready = sem("gap_ready")
        dve_init = sem("dve_init")
        act_init = sem("act_init")


        def xt_start(b):
            return xt[:, b, :] if b < 2 else xt_early[:, b - 2, :]

        half, w2_rows = EXPERTS * DFF // 2, w2t.rearrange("e (f p) c -> p (e f) c", p=P)
        weight_parts = (
            (w1[:, :half], w1t[:, :half]), (w1[:, half:], w1t[:, half:]),
            (w2[:, :half].rearrange("p (f c) -> p f c", c=C), w2_rows[:, :EXPERTS * FT // 2]),
            (w2[:, half:].rearrange("p (f c) -> p f c", c=C), w2_rows[:, EXPERTS * FT // 2:]))

        def unit_heads(w):
            return range(QUADS) if w == 4 else range(2 * (w % 2), 2 * (w % 2) + 2)

        def apply_decay(eng, at, w, tile):
            heads = unit_heads(w)
            part = probs[:, at.ring(2), w, :].rearrange("p (h k) -> p h k", h=len(heads))[:, :, TILE_COLS[tile]]
            weights = wdist[:, at.g * QUADS + heads[0]:at.g * QUADS + heads[-1] + 1, 0:SEQ - tile * P]
            if tile in DVE_TILES:
                return eng.scalar_tensor_tensor(out=part, in0=part, scalar=1.0, in1=weights, op0=ALU.min,
                                                op1=ALU.mult)
            return eng.tensor_tensor(part, part, weights, ALU.mult)

        def add_picked(engine, eng, batches, summed):
            for n, b in enumerate(batches):
                x = x_all[:, b * TILES:(b + 1) * TILES, :]
                eng.wait_ge(picked_loaded[b], 16)
                for k in range(TOPK):
                    engine.tensor_tensor(x, x, picked[:, b * TILES:(b + 1) * TILES, k, :], ALU.add
                                         ).then_inc(summed, 1)
                    eng.wait_ge(summed, TOPK * n + k + 1)

        with nc.Block() as block:
            @block.sync
            def _(sp):
                def x_rows(b):
                    return x_in[b].rearrange("(t p) c -> p t c", p=P)

                sp.dma_start(x_all[:, 0:TILES, :], x_rows(0)).then_inc(first_x_loaded, 16)
                sp.dma_start(w_qkv[:], w_attn).then_inc(consts_dma, 16)
                sp.dma_start(wr[:], wrt).then_inc(consts_dma, 16)
                sp.dma_start(decay_in[:], decay_raw.rearrange("(a h) -> a h", a=1).broadcast_to([P, HEADS])
                             ).then_inc(consts_dma, 16)
                sp.dma_start(wo[:], w_proj).then_inc(consts_dma, 16)
                sp.dma_start(x_all[:, TILES:, :], x_in[1:].rearrange("b (t p) c -> p (b t) c", p=P)
                             ).then_inc(x_loaded, 16)
                sp.wait_ge(slot_table, 2)
                sp.dma_start(rows_dram.rearrange("(s p) c -> p s c", p=P),
                             empty_row[:].rearrange("p (s c) -> p s c", s=1).broadcast_to([P, SLOTS, ROW])
                             ).then_inc(filled, 16)
                sp.wait_ge(zeroed, 4)

                def k_step(at):
                    sp.wait_ge(misc_free, at.misc("K", 1))
                    for quad in range(QUADS):
                        rows = slice(quad * QROWS, (quad + 1) * QROWS)
                        sp.dma_start(k_heads[at.ring(4)][rows, quad, :].bitcast(F32),
                                     k_rows[rows, at.ring(2), :].bitcast(F32)).then_inc(k_loaded, 16)

                def xt_step(at):
                    sp.wait_ge(xt_stored, 16 * (BATCH - 2))
                    sp.wait_ge(misc_free, at.misc_before("K", GROUPS + 1, 1))
                    sp.dma_start(xt[:, at.parity, :],
                                 xt_dram[bass.ds(at.batches(1, -2), 1)].rearrange("b p s -> p (b s)")
                                 ).then_inc(xt_loaded, 16)

                run_prologue({"K": k_step})
                for b in range(2, BATCH):
                    sp.wait_ge(start_xt_ready, b + 1)
                    sp.dma_start(xt_dram[b - 2], xt_early[:, b - 2, :]).then_inc(xt_stored, 16)
                def send_load(at):
                    r = at.ring(2)
                    if at.looped or at.c >= 2:
                        sp.wait_ge(second_sent[r], at.groups(8, -8 * r))
                    sp.wait_ge(rows_ready, 2)
                    sp.dma_start(send_rows[r][:], xn_all[:, bass.ds(at.groups(1), 1), :].rearrange("p a c -> p (a c)")
                                 ).then_inc(send_loaded[r], 16)

                def weights_load(at):
                    last = At(0, NGROUP - GROUPS + at.c)
                    sp.wait_ge(pool_probs, decay_done(last, 0 if 1 in dve_tiles(last) else 1)[1])
                    sp.wait_ge(dve_probs, decay_done(last, 2)[1])
                    sp.dma_start(*weight_parts[at.c]).then_inc(w1_dma if at.c < 2 else w2_dma, 16)

                run_slots(sp, {"K": k_step, "XT": xt_step, "SL": send_load, "WL": weights_load})

                def load_rows(i, j):
                    sp.dma_start(slot_rows[j], rows_dram[bass.ds(i * (RING * P) + j * P, P), :]
                                 ).then_inc(rows_loaded[j], 16)

                sp.wait_ge(rows_sent, 16 * NTILE)
                for sent in second_sent:
                    sp.wait_ge(sent, 8 * NTILE)
                for j in range(RING):
                    load_rows(0, j)
                with sp.Fori(1, SLOTS // RING) as i:
                    for j in range(RING):
                        sp.wait_ge(y_sent[j], i * 16)
                        load_rows(i, j)

                for j in range(RING):
                    sp.wait_ge(y_sent[j], 16 * (SLOTS // RING))
                for b in range(BATCH):
                    sp.dma_start(picked[:, b * TILES:(b + 1) * TILES].rearrange("p t k c -> p t (k c)"),
                                 picked_dram.rearrange("(b t p k) c -> b p t (k c)", b=BATCH, t=TILES, k=TOPK)[b]
                                 ).then_inc(picked_loaded[b], 16)
                for b in range(BATCH):
                    if b in DVE_BATCHES:
                        sp.wait_ge(dve_summed, TOPK * (DVE_BATCHES.index(b) + 1))
                    else:
                        sp.wait_ge(pool_summed, TOPK * (POOL_BATCHES.index(b) + 1))
                    sp.dma_start(out[b].rearrange("(t p) c -> p t c", p=P),
                                 x_all[:, b * TILES:(b + 1) * TILES, :]).then_inc(out_stored, 16)
                sp.wait_ge(out_stored, 16 * BATCH)
                sp.wait_ge(xt_loaded, 16 * (BATCH - 2))

            @block.gpsimd
            def _(pool):
                nc.gpsimd.memset(ident[:], 1.0).then_inc(pool_consts, 1)
                nc.gpsimd.memset(mask_q[:], 0.0).then_inc(pool_consts, 1)
                nc.gpsimd.memset(mask_k[:], 0.0).then_inc(pool_consts, 1)
                nc.gpsimd.memset(minus_half[:], -0.5).then_inc(pool_consts, 1)
                nc.gpsimd.memset(ones[:], 1.0).then_inc(pool_consts, 1)
                nc.gpsimd.memset(empty_row[:], 0.0).then_inc(slot_table, 1)
                pool.wait_ge(slot_table, 1)
                nc.gpsimd.iota(empty_row[:, 0:1].bitcast(I32), pattern=[[0, 1]], base=NOWHERE, channel_multiplier=1
                               ).then_inc(slot_table, 1)
                pool.wait_ge(pool_consts, 5)
                nc.gpsimd.affine_select(out=ident[:], in_=ident[:], compare_op=ALU.is_equal, fill=0.0, base=0,
                                        pattern=[[-1, P]], channel_multiplier=1).then_inc(ident_ready, 1)
                twice = mask_q[:].rearrange("p (a k) -> p a k", a=2)
                nc.gpsimd.affine_select(out=twice, in_=twice, compare_op=ALU.is_ge, fill=NEG, base=0,
                                        pattern=[[0, 2], [-1, P]], channel_multiplier=1).then_inc(ident_ready, 1)
                nc.gpsimd.affine_select(out=mask_k[:], in_=mask_k[:], compare_op=ALU.is_ge, fill=NEG, base=0,
                                        pattern=[[1, P]], channel_multiplier=-1).then_inc(ident_ready, 1)
                nc.gpsimd.iota(dist[:], pattern=[[1, SEQ]], base=0, channel_multiplier=-1,
                               allow_small_or_imprecise_dtypes=True).then_inc(ident_ready, 1)
                nc.gpsimd.iota(rank[:], pattern=[[-1, EXPERTS]], base=EXPERTS, channel_multiplier=0,
                               allow_small_or_imprecise_dtypes=True).then_inc(ident_ready, 1)
                pool.wait_ge(ident_ready, 1)
                nc.gpsimd.tensor_copy(ident_bf[:], ident[:]).then_inc(ident_ready, 1)
                nc.gpsimd.affine_select(out=before[:], in_=ones[:], compare_op=ALU.is_ge, fill=0.0, base=-1,
                                        pattern=[[1, P]], channel_multiplier=-1).then_inc(ident_ready, 1)
                nc.gpsimd.iota(slot_no[:], pattern=[[1, SLOTS]], base=0, channel_multiplier=0,
                               allow_small_or_imprecise_dtypes=True).then_inc(slot_table, 1)
                for k in range(TOPK):
                    nc.gpsimd.iota(row_ids[:, k, :], pattern=[[TOPK * P, NTILE]], base=k, channel_multiplier=TOPK
                                   ).then_inc(slot_table, 1)
                for t in k_heads:
                    nc.gpsimd.memset(t[:].bitcast(F32), 0.0).then_inc(zeroed, 1)

                for n, tiles in enumerate(NORM_PARTS):
                    pool.wait_ge(var_ready, 3 * n + 3)
                    nc.gpsimd.tensor_tensor(rstd[:, tiles], var_eps[:, tiles], minus_half[:, tiles], ALU.pow
                                            ).then_inc(rstd_ready, 1)

                for g in range(GROUPS):
                    pool.wait_ge(wdist_ready, g + 1)
                    w = wdist[:, g * QUADS:(g + 1) * QUADS, 0:P]
                    nc.gpsimd.affine_select(out=w, in_=w, compare_op=ALU.is_ge, fill=0.0, base=0,
                                            pattern=[[0, QUADS], [1, P]], channel_multiplier=-1
                                            ).then_inc(wdist_causal, 1)

                def send_row(row, sent):
                    nc.gpsimd.indirect_dma_start(
                        out=rows_dram, out_offset=bass.IndirectOffsetOnAxis(ap=row[:, 0:1].bitcast(U32), axis=0),
                        in_=row[:, 1:], in_offset=None).then_inc(sent, 16)

                pool.wait_ge(filled, 16)
                pool.wait_ge(rows_ready, 1)
                for t in range(NTILE):
                    send_row(xn_all[:, t, :], rows_sent)

                def p2_step(at, w):
                    tile = {0: 0, 1: 0, 2: 1, 3: 1}.get(w)
                    if tile is None or tile in dve_tiles(at):
                        return
                    if not at.looped and at.c < GROUPS:
                        pool.wait_ge(wdist_causal, at.c + 1)
                    pool.wait_ge(exp_ready, at.groups(P2_UNITS, w + 1))
                    apply_decay(nc.gpsimd, at, w, tile).then_inc(pool_probs, 1)

                def send_step(at):
                    pool.wait_ge(send_loaded[at.ring(2)], at.groups(8, 16 - 8 * at.ring(2)))
                    nc.gpsimd.nop(nofuse=True)
                    send_row(send_rows[at.ring(2)], second_sent[at.ring(2)])

                run_slots(pool, {"P2": p2_step, "SC": send_step})

                def slot(i, j):
                    s = i * SLOTS_UNROLL + j
                    pool.wait_ge(y_ready, s + 1)
                    nc.gpsimd.nop(nofuse=True)
                    nc.gpsimd.indirect_dma_start(
                        out=picked_dram, out_offset=bass.IndirectOffsetOnAxis(
                            ap=slot_rows[j % RING][:, 0:1].bitcast(U32), axis=0),
                        in_=slot_y[j % RING], in_offset=None, bounds_check=last_row, oob_is_err=False
                    ).then_inc(y_sent[j % RING], 16)

                last_row = nc.gpsimd.to_reg(BATCH * SEQ * TOPK - 1)
                with pool.Fori(0, SLOT_LOOPS) as i:
                    for j in range(SLOTS_UNROLL):
                        slot(i, j)
                add_picked(nc.gpsimd, pool, POOL_BATCHES, pool_summed)

            @block.scalar
            def _(act):
                act.wait_ge(dve_init, 2)
                nc.scalar.activation(dec_exp[:], dec_abs[:], ACT.Exp, scale=-1.0).then_inc(act_init, 1)
                act.wait_ge(act_init, 1)
                nc.scalar.activation(dec_log[:], dec_exp[:], ACT.Ln, bias=1.0).then_inc(act_init, 1)
                act.wait_ge(dve_init, 3)
                nc.scalar.activation(log_dist[:], dist[:], ACT.Ln, bias=1.0).then_inc(act_init, 1)
                act.wait_ge(act_init, 3)
                act.wait_ge(decay_ready, 1)
                for h in range(HEADS):
                    last = nc.scalar.activation(wdist[:, h, :], log_dist[:], ACT.Ln, bias=1.0, scale=decay[:, h:h + 1])
                last.then_inc(wdist_log, 1)
                act.wait_ge(wdist_log, 1)

                def decay_exp(g):
                    w = wdist[:, g * QUADS:(g + 1) * QUADS, :]
                    nc.scalar.activation(w, w, ACT.Exp, scale=-1.0).then_inc(wdist_ready, 1)


                def hi_step(kind, hi):
                    def step(at):
                        act.wait_ge(misc_full, at.misc(kind, 1))
                        nc.scalar.activation(hi[:], psM[:], ACT.Copy).then_inc(hi_ready, 1)
                    return step

                def q_step(at):
                    act.wait_ge(misc_full, at.misc("Q", 1))
                    nc.scalar.activation(q_rows[:, at.ring(4), :], psM[:], ACT.Copy).then_inc(misc_free, 1)

                def k_step(at):
                    act.wait_ge(misc_full, at.misc("K", 1))
                    nc.scalar.activation(k_rows[:, at.ring(2), :], psM[:], ACT.Identity,
                                         bias=one_row_k[:, 0:1]).then_inc(misc_free, 1)

                def v_step(at):
                    act.wait_ge(misc_full, at.misc("V", 1))
                    nc.scalar.activation(values[:, at.parity, :, :, 0:HD],
                                         psM[:].rearrange("p (t h d) -> p t h d", t=TILES, h=HEADS),
                                         ACT.Copy).then_inc(misc_free, 1)

                def p2_step(at, w):
                    act.wait_ge(p2_full, at.groups(P2_UNITS, w + 1))
                    nc.scalar.activation(probs[:, at.ring(2), w, :],
                                         ps2[:, (at.c * P2_UNITS + w) % 2].rearrange("p a b -> p (a b)"),
                                         ACT.Exp).then_inc(exp_ready, 1)

                def pv_step(at, chunk):
                    if chunk == 3:
                        act.wait_ge(pv_full, at.groups(1, 1))
                        nc.scalar.activation(o_rows[:, at.ring(2), :], psO[:], ACT.Copy).then_inc(o_ready, 1)

                def yt_step(at):
                    act.wait_ge(misc_full, at.misc("YT", 1))
                    nc.scalar.activation(yt[:], psM[:], ACT.Copy).then_inc(misc_free, 1)

                parts = {"QA": hi_step("QA", q_hi), "KA": hi_step("KA", k_hi), "Q": q_step, "K": k_step,
                         "V": v_step, "P2": p2_step, "PV": pv_step, "YT": yt_step}
                for b in range(BATCH):
                    act.wait_ge(start_xt_full, b + 1)
                    nc.scalar.activation(xt_start(b), ps1[:, b % 2], ACT.Copy).then_inc(start_xt_ready, 1)
                    if b == 0:
                        act.wait_ge(row_masks, 1)
                        run_prologue(parts)
                    if b % 2:
                        decay_exp(b // 2)
                act.wait_ge(logits_full, 1)
                nc.scalar.activation(logits[:], psO[:, 0:NTILE * EXPERTS], ACT.Copy).then_inc(logits_ready, 1)
                act.wait_ge(gates_step, GAP_STEP)
                nc.scalar.activation(gap_exp[:], gap_exp[:], ACT.Exp).then_inc(gap_ready, 1)

                act.wait_ge(xt_stored, 16 * (BATCH - 2))
                act.wait_ge(filled, 16)
                run_slots(act, parts)

                def slot(i, j):
                    s = i * ACT_UNROLL + j
                    act.wait_ge(up_full, s + 1)
                    nc.scalar.activation(hidden[:, j % 2], ps1[:, j % 2], ACT.Silu).then_inc(hidden_ready, 1)

                with act.Fori(0, SLOTS // ACT_UNROLL) as i:
                    for j in range(ACT_UNROLL):
                        slot(i, j)

            @block.vector
            def _(dve):
                nc.vector.memset(values[:], 0.0).then_inc(dve_init, 1)
                dve.wait_ge(consts_dma, 16 * 4)
                nc.vector.tensor_scalar(dec_neg[:], decay_in[:], -1.0, None, ALU.mult).then_inc(row_masks_step, 1)
                dve.wait_ge(row_masks_step, 1)
                nc.vector.tensor_tensor(dec_abs[:], decay_in[:], dec_neg[:], ALU.max).then_inc(dve_init, 1)
                dve.wait_ge(ident_ready, 6)
                nc.vector.tensor_scalar(dist[:], dist[:], 0.0, None, ALU.max).then_inc(dve_init, 1)
                cols = ident[:].rearrange("p (q r) -> p q r", q=QUADS)
                nc.vector.tensor_reduce(one_row_k[:], cols[:, :, 0:2], AX.XY, ALU.add).then_inc(row_masks, 1)
                for t in (q_hi_to, q_lo_to, k_hi_to, k_lo_to):
                    nc.vector.memset(t[:].bitcast(F32), 0.0).then_inc(row_masks_step, 1)
                nc.vector.memset(max_cols[:], 0.0).then_inc(row_masks_step, 1)
                dve.wait_ge(dve_init, 1)
                nc.vector.memset(values[:, :, :, :, HD:HD + 1], 1.0).then_inc(row_masks_step, 1)
                dve.wait_ge(row_masks_step, 7)
                for t, first in ((q_hi_to, ROW_HI), (q_hi_to, ROW_HI2), (q_lo_to, ROW_LO),
                                 (k_hi_to, ROW_HI), (k_hi_to, ROW_LO), (k_lo_to, ROW_HI2)):
                    nc.vector.tensor_copy(t[:].rearrange("p g (q r) -> p (g q) r", q=QUADS)[:, :, first:first + HD],
                                          ident[:].rearrange("p (h d) -> p h d", h=HEADS)).then_inc(w_rows_ready, 1)
                nc.vector.tensor_scalar(w_q[:], w_qkv[:, 0:C], SCALE, None, ALU.mult).then_inc(w_rows_ready, 1)

                dve.wait_ge(act_init, 2)
                nc.vector.scalar_tensor_tensor(out=decay[:], in0=decay_in[:], scalar=0.0, in1=dec_log[:],
                                               op0=ALU.max, op1=ALU.add).then_inc(decay_ready, 1)

                v = nc.vector
                for n, (tiles, loaded) in enumerate(zip(NORM_PARTS, (first_x_loaded, x_loaded))):
                    dve.wait_ge(loaded, 16)
                    for t in range(NTILE)[tiles]:
                        last = v.bn_stats(stats[:, t, :], x_all[:, t, :])
                    last.then_inc(stats_ready, 1)
                    dve.wait_ge(stats_ready, n + 1)
                    even, odd = stats[:, tiles, 0:3], stats[:, tiles, 3:6]
                    m, gap, var = mean[:, tiles], between[:, tiles], var_eps[:, tiles]
                    v.tensor_tensor(m, even[:, :, 1], odd[:, :, 1], ALU.add)
                    v.tensor_tensor(gap, even[:, :, 1], odd[:, :, 1], ALU.subtract)
                    v.tensor_tensor(var, even[:, :, 2], odd[:, :, 2], ALU.add).then_inc(var_ready, 1)
                    dve.wait_ge(var_ready, 3 * n + 1)
                    v.tensor_scalar(m, m, 0.5, None, ALU.mult)
                    v.tensor_tensor(gap, gap, gap, ALU.mult)
                    v.tensor_scalar(var, var, 1.0 / C, EPS, ALU.mult, ALU.add).then_inc(var_ready, 1)
                    dve.wait_ge(var_ready, 3 * n + 2)
                    v.scalar_tensor_tensor(out=var, in0=gap, scalar=0.25, in1=var, op0=ALU.mult, op1=ALU.add
                                           ).then_inc(var_ready, 1)

                def normalise(b):
                    for t in range(b * TILES, (b + 1) * TILES):
                        last = v.tensor_scalar(xn_all[:, t, 3:], x_all[:, t, :], mean[:, t:t + 1],
                                               rstd[:, t:t + 1], ALU.subtract, ALU.mult)
                    last.then_inc(xn_ready, 1)

                def lo_step(number, hi, lo):
                    def step(at):
                        dve.wait_ge(hi_ready, at.batches(2, number))
                        nc.vector.tensor_tensor(lo[:], psM[:], hi[:].bitcast(F32), ALU.subtract).then_inc(misc_free, 1)
                    return step

                all_heads = {"QA": lo_step(2, q_hi, q_lo), "KA": lo_step(1, k_hi, k_lo)}
                dve.wait_ge(rstd_ready, 1)
                normalise(0)
                dve.wait_ge(rstd_ready, 2)
                for b in range(1, BATCH):
                    normalise(b)
                    if b == 2:
                        run_prologue(all_heads)

                done = [0]

                def step(instruction):
                    done[0] += 1
                    instruction.then_inc(gates_step, 1)
                    dve.wait_ge(gates_step, done[0])

                lg = logits[:].rearrange("p (t e) -> p t e", e=EXPERTS)

                def wide(t):
                    return t[:].rearrange("p (t a) -> p t a", a=1).broadcast_to([P, NTILE, EXPERTS])

                ranks = rank[:].rearrange("p (a e) -> p a e", a=1).broadcast_to([P, NTILE, EXPERTS])
                dve.wait_ge(logits_ready, 1)
                dve.wait_ge(ident_ready, 7)

                def first_of_best(src, top, pick):
                    step(v.tensor_reduce(top[:], src, AX.X, ALU.max))
                    step(v.tensor_tensor(pick[:], src, wide(top), ALU.is_equal))
                    step(v.tensor_tensor(pick[:], pick[:], ranks, ALU.mult))
                    step(v.tensor_reduce(best[:], pick[:], AX.X, ALU.max))
                    step(v.tensor_tensor(pick[:], pick[:], wide(best), ALU.is_equal))

                first_of_best(lg, top1, pick1)
                step(v.scalar_tensor_tensor(out=masked[:], in0=pick1[:], scalar=NEG, in1=lg,
                                            op0=ALU.mult, op1=ALU.add))
                first_of_best(masked[:], top2, pick2)
                step(v.tensor_tensor(masked[:], pick1[:], pick2[:], ALU.add))
                assert done[0] == PICKS_STEP
                step(v.tensor_tensor(gap_exp[:], top2[:], top1[:], ALU.subtract))
                assert done[0] == GAP_STEP
                dve.wait_ge(gap_ready, 1)
                step(v.tensor_scalar(gate1[:], gap_exp[:], 1.0, None, ALU.add))
                step(v.reciprocal(gate1[:], gate1[:]))
                step(v.tensor_tensor(gate2[:], gate1[:], gap_exp[:], ALU.mult))

                dve.wait_ge(counts_full, 1)
                within = psO[:, 0:256].rearrange("p (t e) -> p t e", e=EXPERTS)
                totals = psO[:, 256:512].rearrange("p (t e) -> p t e", e=EXPERTS)

                def running_sums(a, b, n):
                    d = 1
                    while d < n:
                        v.tensor_copy(b[:, 0:d], a[:, 0:d])
                        step(v.tensor_tensor(b[:, d:n], a[:, d:n], a[:, 0:n - d], ALU.add))
                        a, b = b, a
                        d *= 2
                    return a, b

                step(v.tensor_copy(sums_a[:], totals))
                sums, spare = running_sums(sums_a, sums_b, NTILE)
                step(v.tensor_scalar(n_slots[:], sums[:, NTILE - 1, :], 1.0 / P, (P - 1.0) / P - (P - 1.0) / (2 * P),
                                     ALU.mult, ALU.add))
                step(v.tensor_scalar(n_slots[:], n_slots[:], TWO23, None, ALU.add))
                step(v.tensor_scalar(n_slots[:], n_slots[:], TWO23, None, ALU.subtract))
                step(v.tensor_copy(ends_a[:], n_slots[:]))
                ends, starts = running_sums(ends_a, ends_b, EXPERTS)
                step(v.tensor_tensor(starts[:], ends[:], n_slots[:], ALU.subtract))
                step(v.tensor_scalar(starts[:], starts[:], float(P), None, ALU.mult))
                step(v.tensor_tensor(spare[:], sums[:], totals, ALU.subtract))
                step(v.tensor_tensor(spare[:], within, spare[:], ALU.add))
                step(v.tensor_tensor(spare[:], spare[:],
                                     starts[:].rearrange("p (a e) -> p a e", a=1).broadcast_to([P, NTILE, EXPERTS]),
                                     ALU.add))
                for k, pick in enumerate((pick1, pick2)):
                    step(v.tensor_tensor(pick[:], pick[:], spare[:], ALU.mult))
                    step(v.tensor_reduce(place[:], pick[:], AX.X, ALU.add))
                    step(v.tensor_copy(places[:, k, :], place[:]))

                def set_rows(k, gate):
                    dve.wait_ge(slot_table, 5)
                    v.tensor_copy(xn_all[:, :, 0].bitcast(I32), places[:, k, :])
                    v.tensor_copy(xn_all[:, :, 1].bitcast(I32), row_ids[:, k, :])
                    v.tensor_copy(xn_all[:, :, 2], gate[:]).then_inc(rows_ready, 1)

                set_rows(0, gate1)

                def spread(t, axis, n):
                    return t.rearrange("p (a b) -> p a b", **{axis: 1}).broadcast_to([P, SLOTS, EXPERTS])

                step(v.tensor_tensor(past[:], spread(slot_no[:], "b", SLOTS), spread(ends[:], "a", EXPERTS), ALU.is_ge))
                step(v.tensor_reduce(slot_expert[:], past[:], AX.X, ALU.add))
                step(v.tensor_scalar(slot_expert[:], slot_expert[:], EXPERTS - 1.0, float(DFF), ALU.min, ALU.mult))
                v.tensor_copy(expert_at[:], slot_expert[:]).then_inc(slot_table, 1)

                def p1_step(at, u0, u1):
                    for u in range(u0, u1):
                        bank = ps1[:, u % 2]
                        r = at.ring(2)
                        dve.wait_ge(p1_full, at.groups(P1_UNITS, u + 1))
                        pair, v = u // 5, u % 5
                        if v < 2:
                            todo = [(bank[:, 0:512], neg_max[:, r, 3, 2 * pair + v:2 * pair + v + 1])]
                        elif v < 4:
                            q = 2 * pair + v - 2
                            todo = [(bank[:, 0:384], neg_max[:, r, 2, q:q + 1]),
                                    (bank[:, 384:512], neg_max[:, r, 0, q:q + 1])]
                        else:
                            todo = [(bank.rearrange("p (h k) -> p h k", h=2),
                                     neg_max[:, r, 1, 2 * pair:2 * pair + 2])]
                        for src, dst in todo:
                            last = nc.vector.tensor_reduce(dst, src, AX.X, ALU.max, negate=True)
                        last.then_inc(p1_free, 1)

                def send_second(at):
                    dve.wait_ge(rows_sent, 16 * NTILE)
                    set_rows(1, gate2)

                def hl_step(at):
                    dve.wait_ge(p1_free, at.groups(P1_UNITS, P1_UNITS))
                    r = at.ring(2)
                    hi = max_cols[:, r, :, :, 0]
                    nc.vector.tensor_copy(hi.bitcast(F32R), neg_max[:, r]).then_inc(max_hi, 1)
                    dve.wait_ge(max_hi, at.groups(1, 1))
                    nc.vector.tensor_tensor(max_cols[:, r, :, :, 1], neg_max[:, r], hi,
                                            ALU.subtract).then_inc(max_ready, 1)

                def mt_step(at):
                    dve.wait_ge(misc_full, at.misc("MT", 1))
                    q = q_rows[:, at.ring(4), :]
                    nc.vector.tensor_tensor(q, psM[:], q.bitcast(F32), ALU.add).then_inc(misc_free, 1)

                def dw_step(at, tiles):
                    if not at.looped and at.c < GROUPS:
                        dve.wait_ge(wdist_causal, at.c + 1)
                    for tile in dve_tiles(at):
                        if tile in tiles:
                            dve.wait_ge(exp_ready, at.groups(P2_UNITS, TILE_UNITS[tile][-1] + 1))
                            for w in TILE_UNITS[tile]:
                                last = apply_decay(nc.vector, at, w, tile)
                            last.then_inc(dve_probs, 1)

                def nt_step(at):
                    dve.wait_ge(misc_full, at.misc("NT", 1))
                    o = psM[:].rearrange("p (t q r) -> p t q r", t=TILES, q=QUADS)
                    nc.vector.reciprocal(rden[:], o[:, :, :, HD]).then_inc(den_ready, 1)
                    dve.wait_ge(den_ready, at.groups(1, 1))
                    c0 = at.g * QUADS * HD
                    nc.vector.tensor_tensor(
                        y[:, at.parity, :, c0:c0 + QUADS * HD].rearrange("p t (q d) -> p t q d", q=QUADS),
                        o[:, :, :, 0:HD],
                        rden[:].rearrange("p t (q a) -> p t q a", a=1).broadcast_to([P, TILES, QUADS, HD]),
                        ALU.mult).then_inc(misc_free, 1)

                def pj_step(at):
                    dve.wait_ge(misc_full, at.misc("PJ", 1))
                    x = x_all[:, bass.ds(at.batches(TILES), TILES), :]
                    nc.vector.tensor_tensor(x, psM[:].rearrange("p (t c) -> p t c", t=TILES), x,
                                            ALU.add).then_inc(misc_free, 1)

                run_slots(dve, {**all_heads, "P1": p1_step, "HL": hl_step, "MT": mt_step, "DW": dw_step,
                                "SR": send_second, "NT": nt_step, "PJ": pj_step})

                def token_copy(i, j):
                    dve.wait_ge(slot_xt_full, i * SLOTS_UNROLL + j + 1)
                    v.tensor_copy(slot_xt[:, j % 2], psM[:, 0:P]).then_inc(slot_xt_ready, 1)

                def slot(i, j, last=False):
                    s = i * SLOTS_UNROLL + j
                    dve.wait_ge(turned_full, s + 1)
                    v.tensor_copy(hidden_t[:, j % 2], ps2[:, 0, j % 2]).then_inc(turned_ready, 1)
                    if not (last and j >= SLOTS_UNROLL - 2):
                        token_copy(i, j + 2)
                    dve.wait_ge(down_full, s + 1)
                    v.tensor_scalar(slot_y[j % RING], ps2[:, 1, j % 2, 0:C], slot_rows[j % RING][:, 1:2], None,
                                    ALU.mult).then_inc(y_ready, 1)

                token_copy(0, 0)
                token_copy(0, 1)
                with dve.Fori(0, SLOT_LOOPS - 1) as i:
                    for j in range(SLOTS_UNROLL):
                        slot(i, j)
                for j in range(SLOTS_UNROLL):
                    slot(SLOT_LOOPS - 1, j, last=True)

                add_picked(nc.vector, dve, DVE_BATCHES, dve_summed)

            @block.tensor
            def _(pe):
                pe.wait_ge(ident_ready, 7)
                pe.wait_ge(w_rows_ready, 7)
                mm = nc.tensor.matmul

                def misc_use(at, kind):
                    if MISC[kind, at.c] or at.looped:
                        pe.wait_ge(misc_free, at.misc(kind))

                def transposes(src):
                    for t in range(TILES):
                        last = nc.tensor.transpose(psM[:, t * P:(t + 1) * P], src(t), ident[:])
                    last.then_inc(misc_full, 1)

                def start_logits(b):
                    pe.wait_ge(start_xt_ready, b + 1)
                    for t in range(TILES):
                        last = mm(psO[:, (b * TILES + t) * EXPERTS:(b * TILES + t + 1) * EXPERTS],
                                  xt_start(b)[:, t * P:(t + 1) * P], wr[:], start=True, stop=True)
                    return last

                def all_heads_step(kind, w):
                    def step(at):
                        misc_use(at, kind)
                        if kind == "KA" and (at.looped or at.c >= 2 * GROUPS):
                            pe.wait_ge(xt_loaded, at.batches(16, -16))
                        mm(psM[:], w, xt[:, at.parity, :], start=True, stop=True).then_inc(misc_full, 1)
                    return step

                def v_step(at):
                    misc_use(at, "V")
                    for t in range(TILES):
                        last = mm(psM[:, t * C:(t + 1) * C], xt[:, at.parity, t * P:(t + 1) * P],
                                  w_qkv[:, 2 * C:3 * C], start=True, stop=True)
                    last.then_inc(misc_full, 1)

                def rows_step(kind, hi_to, hi, lo_to, lo):
                    def step(at):
                        misc_use(at, kind)
                        mm(psM[:], hi_to[:, at.g, :], hi[:], start=True, stop=False)
                        mm(psM[:], lo_to[:, at.g, :], lo[:], start=False, stop=True).then_inc(misc_full, 1)
                    return step

                def p1_step(at, u0, u1):
                    q = q_rows[:, at.ring(4), :]
                    k = k_heads[at.ring(4)]

                    def scores(dst, tile, quad, first=True):
                        n = (tile + 1) * P
                        mm(dst[:, 0:n], q[:, tile * P:n], k[:, quad, 0:n], start=first, stop=False)

                    def mask(dst, blocks):
                        return mm(dst, ident_bf[:], mask_q[:, 0:blocks * P], start=False, stop=True)

                    if u0 == 0:
                        pe.wait_ge(misc_free, at.misc("Q", 1))
                        pe.wait_ge(k_loaded, at.groups(64, 64))
                    for u in range(u0, u1):
                        if at.looped or at.c * P1_UNITS + u >= 2:
                            pe.wait_ge(p1_free, at.groups(P1_UNITS, u - 1))
                        bank = ps1[:, u % 2]
                        pair, v = u // 5, u % 5
                        if v < 2:
                            scores(bank, 3, 2 * pair + v)
                            last = mask(bank[:, 384:512], 1)
                        elif v < 4:
                            scores(bank[:, 0:384], 2, 2 * pair + v - 2)
                            scores(bank[:, 384:512], 0, 2 * pair + v - 2, first=False)
                            last = mask(bank[:, 256:512], 2)
                        else:
                            scores(bank[:, 0:256], 1, 2 * pair)
                            scores(bank[:, 256:512], 1, 2 * pair + 1, first=False)
                            last = mask(bank.rearrange("p (h k) -> p h k", h=2)[:, :, P:2 * P], 2)
                        last.then_inc(p1_full, 1)

                def mt_step(at):
                    misc_use(at, "MT")
                    pe.wait_ge(max_ready, at.groups(1, 1))
                    transposes(lambda t: max_cols[:, at.ring(2), t].rearrange("p q r -> p (q r)"))

                def p2_step(at, w):
                    q = q_rows[:, at.ring(4), :]
                    k = k_heads[at.ring(4)]
                    if w == 0:
                        pe.wait_ge(misc_free, at.misc("MT", 1))
                    if at.looped or at.c * P2_UNITS + w >= 2:
                        pe.wait_ge(exp_ready, at.groups(P2_UNITS, w - 1))
                    pair = ps2[:, (at.c * P2_UNITS + w) % 2]

                    def scores(dst, tile, quad, first=True):
                        a = tile * P
                        return mm(dst, k[:, quad, a:a + P], q[:, a:], start=first, stop=w == 4)

                    def mask(dst):
                        return mm(dst, ident_bf[:], mask_k[:], start=False, stop=True)

                    masks = []
                    for s, quad in enumerate(unit_heads(w)):
                        if w < 2:
                            scores(pair[:, s, :], 0, quad)
                            masks.append(pair[:, s, 0:P])
                        elif w < 4:
                            scores(pair[:, s, 0:384], 1, quad)
                            scores(pair[:, s, 384:512], 3, quad, first=False)
                            masks.append(pair[:, s, 0:P])
                        else:
                            last = scores(pair[:, s // 2, s % 2 * 256:s % 2 * 256 + 256], 2, quad)
                    for dst in masks:
                        last = mask(dst)
                    last.then_inc(p2_full, 1)

                def pv_step(at, chunk):
                    if chunk == 0 and (at.looped or at.c > 0):
                        pe.wait_ge(o_ready, at.groups(1))
                    tile = (0, 1, 3, 2)[chunk]
                    on_dve, done = decay_done(at, tile)
                    pe.wait_ge(dve_probs if on_dve else pool_probs, done)
                    for quad in range(QUADS):
                        unit, a, n = {0: (quad // 2, quad % 2 * 512, 512), 1: (2 + quad // 2, quad % 2 * 512, 384),
                                      3: (2 + quad // 2, quad % 2 * 512 + 384, 128), 2: (4, quad * 256, 256)}[tile]
                        last = mm(psO[quad * QROWS:(quad + 1) * QROWS, tile * P:],
                                  values[:, at.parity, tile, at.g * QUADS + quad, :],
                                  probs[:, at.ring(2), unit, a:a + n], start=(chunk == 0), stop=(chunk == 3))
                    if chunk == 3:
                        last.then_inc(pv_full, 1)

                def nt_step(at):
                    misc_use(at, "NT")
                    pe.wait_ge(o_ready, at.groups(1, 1))
                    transposes(lambda t: o_rows[:, at.ring(2), t * P:(t + 1) * P])

                def yt_step(at):
                    misc_use(at, "YT")
                    transposes(lambda t: y[:, at.parity, t, :])

                def pj_step(at):
                    misc_use(at, "PJ")
                    for t in range(TILES):
                        last = mm(psM[:, t * C:(t + 1) * C], yt[:, t * P:(t + 1) * P], wo[:], start=True, stop=True)
                    last.then_inc(misc_full, 1)

                parts = {"QA": all_heads_step("QA", w_q[:]), "KA": all_heads_step("KA", w_qkv[:, C:2 * C]),
                         "V": v_step, "Q": rows_step("Q", q_hi_to, q_hi, q_lo_to, q_lo),
                         "K": rows_step("K", k_hi_to, k_hi, k_lo_to, k_lo), "P1": p1_step, "MT": mt_step,
                         "P2": p2_step, "PV": pv_step, "NT": nt_step, "YT": yt_step, "PJ": pj_step}
                for b in range(BATCH):
                    pe.wait_ge(xn_ready, b + 1)
                    if b >= 2:
                        pe.wait_ge(start_xt_ready, b - 1)
                    for t in range(TILES):
                        last = nc.tensor.transpose(ps1[:, b % 2, t * P:(t + 1) * P], xn_all[:, b * TILES + t, 3:],
                                                   ident[:])
                    last.then_inc(start_xt_full, 1)
                    if b == 0:
                        pe.wait_ge(start_xt_ready, 1)
                        run_prologue(parts)
                    else:
                        start_logits(b - 1)
                start_logits(BATCH - 1).then_inc(logits_full, 1)
                pe.wait_ge(gates_step, PICKS_STEP)
                picks = masked[:].rearrange("p t e -> p (t e)")
                mm(psO[:, 0:256], before[:], picks, start=True, stop=True)
                mm(psO[:, 256:512], ones[:], picks, start=True, stop=True).then_inc(counts_full, 1)

                run_slots(pe, parts)

                pe.wait_ge(slot_table, 6)
                pe.wait_ge(misc_free, len(MISC))
                pe.wait_ge(exp_ready, P2_ALL)
                pe.wait_ge(p1_free, P1_ALL)

                def positive(s, less):
                    return not isinstance(s, int) or s - less >= 0

                def expert_start(i, j):
                    return nc.tensor.value_load(expert_at[0:1, bass.ds(i * SLOTS_UNROLL + j, 1)], min_val=0,
                                                max_val=(EXPERTS - 1) * DFF)

                def turn_tokens(i, j):
                    s = i * SLOTS_UNROLL + j
                    pe.wait_ge(rows_loaded[j % RING], i * (SLOTS_UNROLL // RING * 16) + (j // RING + 1) * 16)
                    if positive(s, 1):
                        pe.wait_ge(slot_xt_ready, s)
                    nc.tensor.transpose(psM[:, 0:P], slot_rows[j % RING][:, 2:], ident[:]).then_inc(slot_xt_full, 1)

                def up(i, j, at):
                    s = i * SLOTS_UNROLL + j
                    pe.wait_ge(slot_xt_ready, s + 1)
                    if positive(s, 2):
                        pe.wait_ge(hidden_ready, s - 1)
                    mm(ps1[:, j % 2], slot_xt[:, j % 2], w1[:, bass.ds(at, DFF)], start=True, stop=True
                       ).then_inc(up_full, 1)

                def turn_hidden(i, j):
                    s = i * SLOTS_UNROLL + j
                    pe.wait_ge(hidden_ready, s + 1)
                    if positive(s, 2):
                        pe.wait_ge(turned_ready, s - 1)
                    for f in range(FT):
                        last = nc.tensor.transpose(ps2[:, 0, j % 2, f * P:(f + 1) * P],
                                                   hidden[:, j % 2, f * P:(f + 1) * P], ident[:])
                    last.then_inc(turned_full, 1)

                def down(i, j, at):
                    s = i * SLOTS_UNROLL + j
                    pe.wait_ge(turned_ready, s + 1)
                    if positive(s, 2):
                        pe.wait_ge(y_ready, s - 1)
                    for f in range(FT):
                        last = mm(ps2[:, 1, j % 2, 0:C], hidden_t[:, j % 2, f * P:(f + 1) * P],
                                  w2[:, bass.ds(at + f * C, C)], start=(f == 0), stop=(f == FT - 1))
                    last.then_inc(down_full, 1)

                def slots(i, last):
                    starts = [expert_start(i, j) for j in range(2)]
                    for j in range(SLOTS_UNROLL):
                        turn_hidden(i, j)
                        if not (last and j == SLOTS_UNROLL - 1):
                            up(i, j + 1, starts[j + 1])
                            if j + 2 < SLOTS_UNROLL + (not last):
                                starts.append(expert_start(i, j + 2))
                        if not (last and j >= SLOTS_UNROLL - 2):
                            turn_tokens(i, j + 2)
                        down(i, j, starts[j])

                turn_tokens(0, 0)
                turn_tokens(0, 1)
                pe.wait_ge(w1_dma, 32)
                up(0, 0, expert_start(0, 0))
                pe.wait_ge(w2_dma, 32)
                slots(0, False)
                with pe.Fori(1, SLOT_LOOPS - 1) as i:
                    slots(i, False)
                slots(SLOT_LOOPS - 1, True)


def kernel(L0_attn_x, L0_attn_w_attn, L0_attn_w_proj, L0_attn_decay_raw, L0_ffn_W1, L0_ffn_W2, L0_ffn_Wr):
    import numpy as np
    import concourse.bacc as bacc
    from concourse.bass_utils import run_bass_kernel_spmd

    nc = bacc.Bacc("TRN2", target_bir_lowering=False, num_devices=1)
    arrays = {
        "x": np.asarray(L0_attn_x),
        "w_attn": np.asarray(L0_attn_w_attn),
        "w_proj": np.asarray(L0_attn_w_proj),
        "decay_raw": np.asarray(L0_attn_decay_raw),
        "w1t": np.asarray(L0_ffn_W1).transpose(2, 0, 1).reshape(C, EXPERTS * DFF),
        "w2t": np.asarray(L0_ffn_W2).transpose(0, 2, 1),
        "wrt": np.asarray(L0_ffn_Wr).T,
    }
    arrays = {k: np.ascontiguousarray(v) for k, v in arrays.items()}
    args = [nc.dram_tensor(k, v.shape, mybir.dt.from_np(v.dtype), kind="ExternalInput").ap() for k, v in arrays.items()]
    out = nc.dram_tensor("out", (BATCH, SEQ, C), F32, kind="ExternalOutput").ap()
    build(nc, *args, out)
    return run_bass_kernel_spmd(nc, [arrays], core_ids=[0]).results[0]["out"]
```
